# Optimizing a Trainium2 kernel written in Bass

```python
import numpy as np
import jax
import jax.numpy as jnp

def _softmax(x, axis=-1):
    return jax.nn.softmax(x, axis=axis)

def _gelu(x):
    return jax.nn.gelu(x, approximate=True)

def _silu(x):
    return jax.nn.silu(x)

def _sigmoid(x):
    return jax.nn.sigmoid(x)

def _layernorm(x, axis=-1, eps=1e-05):
    m = jnp.mean(x, axis=axis, keepdims=True)
    v = jnp.var(x, axis=axis, keepdims=True)
    return (x - m) / jnp.sqrt(v + eps)

def _scatter_add(tgt, idx, src, axis=0):
    return tgt.at[idx].add(src)

def _segment_sum(src, seg, n):
    return jax.ops.segment_sum(src, seg, n)
kernel_name = 'mk_rec_standalone_d1_rec_r8_14d24b'

def setup_inputs(seed: int=0):
    np.random.seed(seed)
    _w = jnp.asarray

    def _rec_inputs():
        import jax
        import jax.numpy as jnp
        _rk = jax.random.key(seed)
        r_history_ids = jnp.stack([jax.random.randint(jax.random.fold_in(jax.random.fold_in(_rk, 1), 0), (512,), 1, 99997, jnp.int32), jax.random.randint(jax.random.fold_in(jax.random.fold_in(_rk, 1), 1), (512,), 22, 99993, jnp.int32), jax.random.randint(jax.random.fold_in(jax.random.fold_in(_rk, 1), 2), (512,), 29, 99986, jnp.int32), jax.random.randint(jax.random.fold_in(jax.random.fold_in(_rk, 1), 3), (512,), 0, 99978, jnp.int32), jax.random.randint(jax.random.fold_in(jax.random.fold_in(_rk, 1), 4), (512,), 18, 99970, jnp.int32), jax.random.randint(jax.random.fold_in(jax.random.fold_in(_rk, 1), 5), (512,), 15, 99991, jnp.int32), jax.random.randint(jax.random.fold_in(jax.random.fold_in(_rk, 1), 6), (512,), 35, 99965, jnp.int32), jax.random.randint(jax.random.fold_in(jax.random.fold_in(_rk, 1), 7), (512,), 21, 99979, jnp.int32), jax.random.randint(jax.random.fold_in(jax.random.fold_in(_rk, 1), 8), (512,), 18, 99957, jnp.int32), jax.random.randint(jax.random.fold_in(jax.random.fold_in(_rk, 1), 9), (512,), 13, 99931, jnp.int32), jax.random.randint(jax.random.fold_in(jax.random.fold_in(_rk, 1), 10), (512,), 29, 99993, jnp.int32), jax.random.randint(jax.random.fold_in(jax.random.fold_in(_rk, 1), 11), (512,), 105, 99966, jnp.int32), jax.random.randint(jax.random.fold_in(jax.random.fold_in(_rk, 1), 12), (512,), 12, 99998, jnp.int32), jax.random.randint(jax.random.fold_in(jax.random.fold_in(_rk, 1), 13), (512,), 44, 99970, jnp.int32), jax.random.randint(jax.random.fold_in(jax.random.fold_in(_rk, 1), 14), (512,), 7, 99975, jnp.int32), jax.random.randint(jax.random.fold_in(jax.random.fold_in(_rk, 1), 15), (512,), 94, 99979, jnp.int32), jax.random.randint(jax.random.fold_in(jax.random.fold_in(_rk, 1), 16), (512,), 28, 12499, jnp.int32), jax.random.randint(jax.random.fold_in(jax.random.fold_in(_rk, 1), 17), (512,), 4, 99978, jnp.int32), jax.random.randint(jax.random.fold_in(jax.random.fold_in(_rk, 1), 18), (512,), 44, 99989, jnp.int32), jax.random.randint(jax.random.fold_in(jax.random.fold_in(_rk, 1), 19), (512,), 6, 99959, jnp.int32), jax.random.randint(jax.random.fold_in(jax.random.fold_in(_rk, 1), 20), (512,), 9, 99988, jnp.int32), jax.random.randint(jax.random.fold_in(jax.random.fold_in(_rk, 1), 21), (512,), 15, 99998, jnp.int32), jax.random.randint(jax.random.fold_in(jax.random.fold_in(_rk, 1), 22), (512,), 73, 99961, jnp.int32), jax.random.randint(jax.random.fold_in(jax.random.fold_in(_rk, 1), 23), (512,), 11, 99978, jnp.int32), jax.random.randint(jax.random.fold_in(jax.random.fold_in(_rk, 1), 24), (512,), 62, 99994, jnp.int32), jax.random.randint(jax.random.fold_in(jax.random.fold_in(_rk, 1), 25), (512,), 35, 12494, jnp.int32), jax.random.randint(jax.random.fold_in(jax.random.fold_in(_rk, 1), 26), (512,), 23, 99961, jnp.int32), jax.random.randint(jax.random.fold_in(jax.random.fold_in(_rk, 1), 27), (512,), 5, 99988, jnp.int32), jax.random.randint(jax.random.fold_in(jax.random.fold_in(_rk, 1), 28), (512,), 32, 99993, jnp.int32), jax.random.randint(jax.random.fold_in(jax.random.fold_in(_rk, 1), 29), (512,), 36, 99983, jnp.int32), jax.random.randint(jax.random.fold_in(jax.random.fold_in(_rk, 1), 30), (512,), 100, 99972, jnp.int32), jax.random.randint(jax.random.fold_in(jax.random.fold_in(_rk, 1), 31), (512,), 39, 99943, jnp.int32), jax.random.randint(jax.random.fold_in(jax.random.fold_in(_rk, 1), 32), (512,), 10, 99965, jnp.int32), jax.random.randint(jax.random.fold_in(jax.random.fold_in(_rk, 1), 33), (512,), 43, 99966, jnp.int32), jax.random.randint(jax.random.fold_in(jax.random.fold_in(_rk, 1), 34), (512,), 8, 99997, jnp.int32), jax.random.randint(jax.random.fold_in(jax.random.fold_in(_rk, 1), 35), (512,), 32, 99998, jnp.int32), jax.random.randint(jax.random.fold_in(jax.random.fold_in(_rk, 1), 36), (512,), 9, 99938, jnp.int32), jax.random.randint(jax.random.fold_in(jax.random.fold_in(_rk, 1), 37), (512,), 54, 12498, jnp.int32), jax.random.randint(jax.random.fold_in(jax.random.fold_in(_rk, 1), 38), (512,), 27, 99995, jnp.int32), jax.random.randint(jax.random.fold_in(jax.random.fold_in(_rk, 1), 39), (512,), 14, 99965, jnp.int32), jax.random.randint(jax.random.fold_in(jax.random.fold_in(_rk, 1), 40), (512,), 20, 99998, jnp.int32), jax.random.randint(jax.random.fold_in(jax.random.fold_in(_rk, 1), 41), (512,), 20, 99878, jnp.int32), jax.random.randint(jax.random.fold_in(jax.random.fold_in(_rk, 1), 42), (512,), 51, 99990, jnp.int32), jax.random.randint(jax.random.fold_in(jax.random.fold_in(_rk, 1), 43), (512,), 37, 99997, jnp.int32), jax.random.randint(jax.random.fold_in(jax.random.fold_in(_rk, 1), 44), (512,), 22, 99999, jnp.int32), jax.random.randint(jax.random.fold_in(jax.random.fold_in(_rk, 1), 45), (512,), 12, 99995, jnp.int32), jax.random.randint(jax.random.fold_in(jax.random.fold_in(_rk, 1), 46), (512,), 41, 99974, jnp.int32), jax.random.randint(jax.random.fold_in(jax.random.fold_in(_rk, 1), 47), (512,), 34, 99994, jnp.int32), jax.random.randint(jax.random.fold_in(jax.random.fold_in(_rk, 1), 48), (512,), 125, 99995, jnp.int32), jax.random.randint(jax.random.fold_in(jax.random.fold_in(_rk, 1), 49), (512,), 20, 99994, jnp.int32), jax.random.randint(jax.random.fold_in(jax.random.fold_in(_rk, 1), 50), (512,), 98, 99989, jnp.int32), jax.random.randint(jax.random.fold_in(jax.random.fold_in(_rk, 1), 51), (512,), 37, 12498, jnp.int32), jax.random.randint(jax.random.fold_in(jax.random.fold_in(_rk, 1), 52), (512,), 4, 99979, jnp.int32), jax.random.randint(jax.random.fold_in(jax.random.fold_in(_rk, 1), 53), (512,), 2, 99963, jnp.int32), jax.random.randint(jax.random.fold_in(jax.random.fold_in(_rk, 1), 54), (512,), 52, 99995, jnp.int32), jax.random.randint(jax.random.fold_in(jax.random.fold_in(_rk, 1), 55), (512,), 67, 99994, jnp.int32), jax.random.randint(jax.random.fold_in(jax.random.fold_in(_rk, 1), 56), (512,), 1, 99994, jnp.int32), jax.random.randint(jax.random.fold_in(jax.random.fold_in(_rk, 1), 57), (512,), 31, 99997, jnp.int32), jax.random.randint(jax.random.fold_in(jax.random.fold_in(_rk, 1), 58), (512,), 51, 99996, jnp.int32), jax.random.randint(jax.random.fold_in(jax.random.fold_in(_rk, 1), 59), (512,), 21, 99983, jnp.int32), jax.random.randint(jax.random.fold_in(jax.random.fold_in(_rk, 1), 60), (512,), 39, 99959, jnp.int32), jax.random.randint(jax.random.fold_in(jax.random.fold_in(_rk, 1), 61), (512,), 4, 99972, jnp.int32), jax.random.randint(jax.random.fold_in(jax.random.fold_in(_rk, 1), 62), (512,), 11, 99995, jnp.int32), jax.random.randint(jax.random.fold_in(jax.random.fold_in(_rk, 1), 63), (512,), 31, 12498, jnp.int32), jax.random.randint(jax.random.fold_in(jax.random.fold_in(_rk, 1), 64), (512,), 14, 99997, jnp.int32), jax.random.randint(jax.random.fold_in(jax.random.fold_in(_rk, 1), 65), (512,), 42, 12496, jnp.int32), jax.random.randint(jax.random.fold_in(jax.random.fold_in(_rk, 1), 66), (512,), 33, 99986, jnp.int32), jax.random.randint(jax.random.fold_in(jax.random.fold_in(_rk, 1), 67), (512,), 14, 99973, jnp.int32), jax.random.randint(jax.random.fold_in(jax.random.fold_in(_rk, 1), 68), (512,), 11, 99989, jnp.int32), jax.random.randint(jax.random.fold_in(jax.random.fold_in(_rk, 1), 69), (512,), 67, 99973, jnp.int32), jax.random.randint(jax.random.fold_in(jax.random.fold_in(_rk, 1), 70), (512,), 1, 99982, jnp.int32), jax.random.randint(jax.random.fold_in(jax.random.fold_in(_rk, 1), 71), (512,), 6, 99994, jnp.int32), jax.random.randint(jax.random.fold_in(jax.random.fold_in(_rk, 1), 72), (512,), 81, 99999, jnp.int32), jax.random.randint(jax.random.fold_in(jax.random.fold_in(_rk, 1), 73), (512,), 3, 99985, jnp.int32), jax.random.randint(jax.random.fold_in(jax.random.fold_in(_rk, 1), 74), (512,), 5, 99957, jnp.int32), jax.random.randint(jax.random.fold_in(jax.random.fold_in(_rk, 1), 75), (512,), 2, 99980, jnp.int32), jax.random.randint(jax.random.fold_in(jax.random.fold_in(_rk, 1), 76), (512,), 39, 99922, jnp.int32), jax.random.randint(jax.random.fold_in(jax.random.fold_in(_rk, 1), 77), (512,), 0, 99964, jnp.int32), jax.random.randint(jax.random.fold_in(jax.random.fold_in(_rk, 1), 78), (512,), 7, 99993, jnp.int32), jax.random.randint(jax.random.fold_in(jax.random.fold_in(_rk, 1), 79), (512,), 39, 99994, jnp.int32), jax.random.randint(jax.random.fold_in(jax.random.fold_in(_rk, 1), 80), (512,), 3, 99991, jnp.int32), jax.random.randint(jax.random.fold_in(jax.random.fold_in(_rk, 1), 81), (512,), 6, 99982, jnp.int32), jax.random.randint(jax.random.fold_in(jax.random.fold_in(_rk, 1), 82), (512,), 50, 99997, jnp.int32), jax.random.randint(jax.random.fold_in(jax.random.fold_in(_rk, 1), 83), (512,), 3, 99991, jnp.int32), jax.random.randint(jax.random.fold_in(jax.random.fold_in(_rk, 1), 84), (512,), 95, 99948, jnp.int32), jax.random.randint(jax.random.fold_in(jax.random.fold_in(_rk, 1), 85), (512,), 19, 99963, jnp.int32), jax.random.randint(jax.random.fold_in(jax.random.fold_in(_rk, 1), 86), (512,), 62, 99996, jnp.int32), jax.random.randint(jax.random.fold_in(jax.random.fold_in(_rk, 1), 87), (512,), 68, 99947, jnp.int32), jax.random.randint(jax.random.fold_in(jax.random.fold_in(_rk, 1), 88), (512,), 38, 99926, jnp.int32), jax.random.randint(jax.random.fold_in(jax.random.fold_in(_rk, 1), 89), (512,), 10, 99981, jnp.int32), jax.random.randint(jax.random.fold_in(jax.random.fold_in(_rk, 1), 90), (512,), 19, 99986, jnp.int32), jax.random.randint(jax.random.fold_in(jax.random.fold_in(_rk, 1), 91), (512,), 1, 99999, jnp.int32), jax.random.randint(jax.random.fold_in(jax.random.fold_in(_rk, 1), 92), (512,), 8, 99905, jnp.int32), jax.random.randint(jax.random.fold_in(jax.random.fold_in(_rk, 1), 93), (512,), 2, 99980, jnp.int32), jax.random.randint(jax.random.fold_in(jax.random.fold_in(_rk, 1), 94), (512,), 0, 12497, jnp.int32), jax.random.randint(jax.random.fold_in(jax.random.fold_in(_rk, 1), 95), (512,), 5, 12499, jnp.int32), jax.random.randint(jax.random.fold_in(jax.random.fold_in(_rk, 1), 96), (512,), 63, 99951, jnp.int32), jax.random.randint(jax.random.fold_in(jax.random.fold_in(_rk, 1), 97), (512,), 10, 99967, jnp.int32), jax.random.randint(jax.random.fold_in(jax.random.fold_in(_rk, 1), 98), (512,), 12, 99986, jnp.int32), jax.random.randint(jax.random.fold_in(jax.random.fold_in(_rk, 1), 99), (512,), 0, 99971, jnp.int32), jax.random.randint(jax.random.fold_in(jax.random.fold_in(_rk, 1), 100), (512,), 30, 99986, jnp.int32), jax.random.randint(jax.random.fold_in(jax.random.fold_in(_rk, 1), 101), (512,), 55, 12500, jnp.int32), jax.random.randint(jax.random.fold_in(jax.random.fold_in(_rk, 1), 102), (512,), 34, 99965, jnp.int32), jax.random.randint(jax.random.fold_in(jax.random.fold_in(_rk, 1), 103), (512,), 28, 99987, jnp.int32), jax.random.randint(jax.random.fold_in(jax.random.fold_in(_rk, 1), 104), (512,), 17, 99979, jnp.int32), jax.random.randint(jax.random.fold_in(jax.random.fold_in(_rk, 1), 105), (512,), 29, 99890, jnp.int32), jax.random.randint(jax.random.fold_in(jax.random.fold_in(_rk, 1), 106), (512,), 41, 12500, jnp.int32), jax.random.randint(jax.random.fold_in(jax.random.fold_in(_rk, 1), 107), (512,), 13, 99978, jnp.int32), jax.random.randint(jax.random.fold_in(jax.random.fold_in(_rk, 1), 108), (512,), 36, 99988, jnp.int32), jax.random.randint(jax.random.fold_in(jax.random.fold_in(_rk, 1), 109), (512,), 15, 99961, jnp.int32), jax.random.randint(jax.random.fold_in(jax.random.fold_in(_rk, 1), 110), (512,), 4, 99988, jnp.int32), jax.random.randint(jax.random.fold_in(jax.random.fold_in(_rk, 1), 111), (512,), 33, 99965, jnp.int32), jax.random.randint(jax.random.fold_in(jax.random.fold_in(_rk, 1), 112), (512,), 39, 99990, jnp.int32), jax.random.randint(jax.random.fold_in(jax.random.fold_in(_rk, 1), 113), (512,), 22, 99985, jnp.int32), jax.random.randint(jax.random.fold_in(jax.random.fold_in(_rk, 1), 114), (512,), 3, 99982, jnp.int32), jax.random.randint(jax.random.fold_in(jax.random.fold_in(_rk, 1), 115), (512,), 81, 99962, jnp.int32), jax.random.randint(jax.random.fold_in(jax.random.fold_in(_rk, 1), 116), (512,), 15, 99967, jnp.int32), jax.random.randint(jax.random.fold_in(jax.random.fold_in(_rk, 1), 117), (512,), 17, 99988, jnp.int32), jax.random.randint(jax.random.fold_in(jax.random.fold_in(_rk, 1), 118), (512,), 0, 99993, jnp.int32), jax.random.randint(jax.random.fold_in(jax.random.fold_in(_rk, 1), 119), (512,), 10, 99973, jnp.int32), jax.random.randint(jax.random.fold_in(jax.random.fold_in(_rk, 1), 120), (512,), 16, 99932, jnp.int32), jax.random.randint(jax.random.fold_in(jax.random.fold_in(_rk, 1), 121), (512,), 5, 99997, jnp.int32), jax.random.randint(jax.random.fold_in(jax.random.fold_in(_rk, 1), 122), (512,), 0, 99980, jnp.int32), jax.random.randint(jax.random.fold_in(jax.random.fold_in(_rk, 1), 123), (512,), 7, 12494, jnp.int32), jax.random.randint(jax.random.fold_in(jax.random.fold_in(_rk, 1), 124), (512,), 12, 99966, jnp.int32), jax.random.randint(jax.random.fold_in(jax.random.fold_in(_rk, 1), 125), (512,), 62, 99910, jnp.int32), jax.random.randint(jax.random.fold_in(jax.random.fold_in(_rk, 1), 126), (512,), 31, 99932, jnp.int32), jax.random.randint(jax.random.fold_in(jax.random.fold_in(_rk, 1), 127), (512,), 13, 99995, jnp.int32), jax.random.randint(jax.random.fold_in(jax.random.fold_in(_rk, 1), 128), (512,), 22, 99983, jnp.int32), jax.random.randint(jax.random.fold_in(jax.random.fold_in(_rk, 1), 129), (512,), 97, 99854, jnp.int32), jax.random.randint(jax.random.fold_in(jax.random.fold_in(_rk, 1), 130), (512,), 21, 99938, jnp.int32), jax.random.randint(jax.random.fold_in(jax.random.fold_in(_rk, 1), 131), (512,), 2, 99964, jnp.int32), jax.random.randint(jax.random.fold_in(jax.random.fold_in(_rk, 1), 132), (512,), 22, 99997, jnp.int32), jax.random.randint(jax.random.fold_in(jax.random.fold_in(_rk, 1), 133), (512,), 17, 99988, jnp.int32), jax.random.randint(jax.random.fold_in(jax.random.fold_in(_rk, 1), 134), (512,), 19, 99999, jnp.int32), jax.random.randint(jax.random.fold_in(jax.random.fold_in(_rk, 1), 135), (512,), 35, 12500, jnp.int32), jax.random.randint(jax.random.fold_in(jax.random.fold_in(_rk, 1), 136), (512,), 2, 99994, jnp.int32), jax.random.randint(jax.random.fold_in(jax.random.fold_in(_rk, 1), 137), (512,), 53, 12499, jnp.int32), jax.random.randint(jax.random.fold_in(jax.random.fold_in(_rk, 1), 138), (512,), 23, 99953, jnp.int32), jax.random.randint(jax.random.fold_in(jax.random.fold_in(_rk, 1), 139), (512,), 2, 99978, jnp.int32), jax.random.randint(jax.random.fold_in(jax.random.fold_in(_rk, 1), 140), (512,), 12, 99981, jnp.int32), jax.random.randint(jax.random.fold_in(jax.random.fold_in(_rk, 1), 141), (512,), 92, 99982, jnp.int32), jax.random.randint(jax.random.fold_in(jax.random.fold_in(_rk, 1), 142), (512,), 41, 12498, jnp.int32), jax.random.randint(jax.random.fold_in(jax.random.fold_in(_rk, 1), 143), (512,), 2, 99910, jnp.int32), jax.random.randint(jax.random.fold_in(jax.random.fold_in(_rk, 1), 144), (512,), 5, 99972, jnp.int32), jax.random.randint(jax.random.fold_in(jax.random.fold_in(_rk, 1), 145), (512,), 14, 99950, jnp.int32), jax.random.randint(jax.random.fold_in(jax.random.fold_in(_rk, 1), 146), (512,), 11, 99964, jnp.int32), jax.random.randint(jax.random.fold_in(jax.random.fold_in(_rk, 1), 147), (512,), 27, 99993, jnp.int32), jax.random.randint(jax.random.fold_in(jax.random.fold_in(_rk, 1), 148), (512,), 3, 12498, jnp.int32), jax.random.randint(jax.random.fold_in(jax.random.fold_in(_rk, 1), 149), (512,), 8, 99971, jnp.int32), jax.random.randint(jax.random.fold_in(jax.random.fold_in(_rk, 1), 150), (512,), 82, 99919, jnp.int32), jax.random.randint(jax.random.fold_in(jax.random.fold_in(_rk, 1), 151), (512,), 9, 99999, jnp.int32), jax.random.randint(jax.random.fold_in(jax.random.fold_in(_rk, 1), 152), (512,), 3, 99957, jnp.int32), jax.random.randint(jax.random.fold_in(jax.random.fold_in(_rk, 1), 153), (512,), 19, 99977, jnp.int32), jax.random.randint(jax.random.fold_in(jax.random.fold_in(_rk, 1), 154), (512,), 18, 99978, jnp.int32), jax.random.randint(jax.random.fold_in(jax.random.fold_in(_rk, 1), 155), (512,), 50, 99988, jnp.int32), jax.random.randint(jax.random.fold_in(jax.random.fold_in(_rk, 1), 156), (512,), 2, 99999, jnp.int32), jax.random.randint(jax.random.fold_in(jax.random.fold_in(_rk, 1), 157), (512,), 40, 12498, jnp.int32), jax.random.randint(jax.random.fold_in(jax.random.fold_in(_rk, 1), 158), (512,), 20, 99933, jnp.int32), jax.random.randint(jax.random.fold_in(jax.random.fold_in(_rk, 1), 159), (512,), 9, 99950, jnp.int32), jax.random.randint(jax.random.fold_in(jax.random.fold_in(_rk, 1), 160), (512,), 38, 99985, jnp.int32), jax.random.randint(jax.random.fold_in(jax.random.fold_in(_rk, 1), 161), (512,), 31, 99998, jnp.int32), jax.random.randint(jax.random.fold_in(jax.random.fold_in(_rk, 1), 162), (512,), 8, 99986, jnp.int32), jax.random.randint(jax.random.fold_in(jax.random.fold_in(_rk, 1), 163), (512,), 6, 99963, jnp.int32), jax.random.randint(jax.random.fold_in(jax.random.fold_in(_rk, 1), 164), (512,), 15, 99886, jnp.int32), jax.random.randint(jax.random.fold_in(jax.random.fold_in(_rk, 1), 165), (512,), 30, 99941, jnp.int32), jax.random.randint(jax.random.fold_in(jax.random.fold_in(_rk, 1), 166), (512,), 10, 99988, jnp.int32), jax.random.randint(jax.random.fold_in(jax.random.fold_in(_rk, 1), 167), (512,), 0, 99970, jnp.int32), jax.random.randint(jax.random.fold_in(jax.random.fold_in(_rk, 1), 168), (512,), 30, 99998, jnp.int32), jax.random.randint(jax.random.fold_in(jax.random.fold_in(_rk, 1), 169), (512,), 61, 99965, jnp.int32), jax.random.randint(jax.random.fold_in(jax.random.fold_in(_rk, 1), 170), (512,), 51, 99987, jnp.int32), jax.random.randint(jax.random.fold_in(jax.random.fold_in(_rk, 1), 171), (512,), 16, 12500, jnp.int32), jax.random.randint(jax.random.fold_in(jax.random.fold_in(_rk, 1), 172), (512,), 17, 99962, jnp.int32), jax.random.randint(jax.random.fold_in(jax.random.fold_in(_rk, 1), 173), (512,), 49, 99969, jnp.int32), jax.random.randint(jax.random.fold_in(jax.random.fold_in(_rk, 1), 174), (512,), 26, 99916, jnp.int32), jax.random.randint(jax.random.fold_in(jax.random.fold_in(_rk, 1), 175), (512,), 10, 99958, jnp.int32), jax.random.randint(jax.random.fold_in(jax.random.fold_in(_rk, 1), 176), (512,), 1, 99986, jnp.int32), jax.random.randint(jax.random.fold_in(jax.random.fold_in(_rk, 1), 177), (512,), 0, 99990, jnp.int32), jax.random.randint(jax.random.fold_in(jax.random.fold_in(_rk, 1), 178), (512,), 68, 99957, jnp.int32), jax.random.randint(jax.random.fold_in(jax.random.fold_in(_rk, 1), 179), (512,), 4, 99996, jnp.int32), jax.random.randint(jax.random.fold_in(jax.random.fold_in(_rk, 1), 180), (512,), 4, 99979, jnp.int32), jax.random.randint(jax.random.fold_in(jax.random.fold_in(_rk, 1), 181), (512,), 48, 99973, jnp.int32), jax.random.randint(jax.random.fold_in(jax.random.fold_in(_rk, 1), 182), (512,), 7, 99982, jnp.int32), jax.random.randint(jax.random.fold_in(jax.random.fold_in(_rk, 1), 183), (512,), 65, 99977, jnp.int32), jax.random.randint(jax.random.fold_in(jax.random.fold_in(_rk, 1), 184), (512,), 13, 99988, jnp.int32), jax.random.randint(jax.random.fold_in(jax.random.fold_in(_rk, 1), 185), (512,), 1, 99970, jnp.int32), jax.random.randint(jax.random.fold_in(jax.random.fold_in(_rk, 1), 186), (512,), 5, 99994, jnp.int32), jax.random.randint(jax.random.fold_in(jax.random.fold_in(_rk, 1), 187), (512,), 8, 12500, jnp.int32), jax.random.randint(jax.random.fold_in(jax.random.fold_in(_rk, 1), 188), (512,), 9, 99998, jnp.int32), jax.random.randint(jax.random.fold_in(jax.random.fold_in(_rk, 1), 189), (512,), 58, 99999, jnp.int32), jax.random.randint(jax.random.fold_in(jax.random.fold_in(_rk, 1), 190), (512,), 7, 99969, jnp.int32), jax.random.randint(jax.random.fold_in(jax.random.fold_in(_rk, 1), 191), (512,), 14, 99969, jnp.int32), jax.random.randint(jax.random.fold_in(jax.random.fold_in(_rk, 1), 192), (512,), 2, 99982, jnp.int32), jax.random.randint(jax.random.fold_in(jax.random.fold_in(_rk, 1), 193), (512,), 23, 99994, jnp.int32), jax.random.randint(jax.random.fold_in(jax.random.fold_in(_rk, 1), 194), (512,), 12, 12486, jnp.int32), jax.random.randint(jax.random.fold_in(jax.random.fold_in(_rk, 1), 195), (512,), 43, 99977, jnp.int32), jax.random.randint(jax.random.fold_in(jax.random.fold_in(_rk, 1), 196), (512,), 8, 99973, jnp.int32), jax.random.randint(jax.random.fold_in(jax.random.fold_in(_rk, 1), 197), (512,), 34, 99996, jnp.int32), jax.random.randint(jax.random.fold_in(jax.random.fold_in(_rk, 1), 198), (512,), 6, 99997, jnp.int32), jax.random.randint(jax.random.fold_in(jax.random.fold_in(_rk, 1), 199), (512,), 0, 99989, jnp.int32)], axis=1)
        r_history_mask = jax.random.bernoulli(jax.random.fold_in(_rk, 2), 0.4988, (512, 200))
        r_target_ids = jax.random.randint(jax.random.fold_in(_rk, 3), (512,), 18, 99955, jnp.int32)
        return (r_history_ids, r_history_mask, r_target_ids)
    r_history_ids, r_history_mask, r_target_ids = _rec_inputs()

    def _L0_rec_setup():
        import jax, jax.numpy as jnp
        import numpy as np
        B, T, D = (512, 200, 64)
        V, HA, HP = (12500, 128, 128)

        def _xavier(k, fan_in, fan_out):
            lim = np.sqrt(6.0 / (fan_in + fan_out)).astype(np.float32)
            return jax.random.uniform(k, (fan_in, fan_out), minval=-lim, maxval=lim, dtype=jnp.float32)
        key = jax.random.key(seed)
        ks = jax.random.split(key, 8)
        history_ids = jax.random.randint(ks[0], (B, T), 0, V)
        history_mask = jax.random.randint(ks[1], (B, T), 0, 2) > 0
        target_ids = jax.random.randint(ks[2], (B,), 0, V)
        emb = (0.01 * jax.random.normal(ks[3], (V, D), dtype=jnp.float32)).at[0].set(0.0)
        W1a = _xavier(ks[4], 4 * D, HA)
        b1a = jnp.zeros((HA,), jnp.float32)
        W2a = _xavier(ks[5], HA, 1)
        b2a = jnp.zeros((1,), jnp.float32)
        W1p = _xavier(ks[6], 4 * D, HP)
        b1p = jnp.zeros((HP,), jnp.float32)
        W2p = _xavier(ks[7], HP, 1)
        b2p = jnp.zeros((1,), jnp.float32)
        return dict(history_ids=history_ids, history_mask=history_mask, target_ids=target_ids, emb=emb, W1a=W1a, b1a=b1a, W2a=W2a, b2a=b2a, W1p=W1p, b1p=b1p, W2p=W2p, b2p=b2p)
    _L0_rec_all = _L0_rec_setup()
    _L0_rec_in = {k: v for k, v in _L0_rec_all.items() if k in ('emb', 'W1a', 'b1a', 'W2a', 'b2a', 'W1p', 'b1p', 'W2p', 'b2p')}
    del _L0_rec_all
    return {'r_history_ids': r_history_ids, 'r_history_mask': r_history_mask, 'r_target_ids': r_target_ids, 'L0_rec_emb': _L0_rec_in['emb'], 'L0_rec_W1a': _L0_rec_in['W1a'], 'L0_rec_b1a': _L0_rec_in['b1a'], 'L0_rec_W2a': _L0_rec_in['W2a'], 'L0_rec_b2a': _L0_rec_in['b2a'], 'L0_rec_W1p': _L0_rec_in['W1p'], 'L0_rec_b1p': _L0_rec_in['b1p'], 'L0_rec_W2p': _L0_rec_in['W2p'], 'L0_rec_b2p': _L0_rec_in['b2p']}

def reference(r_history_ids, r_history_mask, r_target_ids, L0_rec_emb, L0_rec_W1a, L0_rec_b1a, L0_rec_W2a, L0_rec_b2a, L0_rec_W1p, L0_rec_b1p, L0_rec_W2p, L0_rec_b2p):
    import jax
    import jax.numpy as jnp

    def _L0_rec_ref(history_ids, history_mask, target_ids, emb, W1a, b1a, W2a, b2a, W1p, b1p, W2p, b2p):
        import jax, jax.numpy as jnp
        import numpy as np
        B, T, D = (512, 200, 64)
        V, HA, HP = (12500, 128, 128)

        def _xavier(k, fan_in, fan_out):
            lim = np.sqrt(6.0 / (fan_in + fan_out)).astype(np.float32)
            return jax.random.uniform(k, (fan_in, fan_out), minval=-lim, maxval=lim, dtype=jnp.float32)
        h = emb[history_ids]
        t = emb[target_ids]
        te = jnp.broadcast_to(t[:, None, :], h.shape)
        attn_in = jnp.concatenate([h, te, h - te, h * te], axis=-1)
        scores = (jax.nn.relu(attn_in @ W1a + b1a) @ W2a + b2a)[..., 0]
        scores = jnp.where(history_mask, scores, -jnp.inf)
        all_invalid = ~history_mask.any(axis=1)
        scores = jnp.where(all_invalid[:, None], 0.0, scores)
        w = jax.nn.softmax(scores, axis=1) * history_mask.astype(scores.dtype)
        w = w / jnp.maximum(w.sum(axis=1, keepdims=True), 1e-08)
        u = jnp.einsum('bt,btd->bd', w, h)
        pred_in = jnp.concatenate([u, t, u - t, u * t], axis=-1)
        logits = (jax.nn.relu(pred_in @ W1p + b1p) @ W2p + b2p)[..., 0]
        return logits
    y = _L0_rec_ref(r_history_ids, r_history_mask, r_target_ids, L0_rec_emb, L0_rec_W1a, L0_rec_b1a, L0_rec_W2a, L0_rec_b2a, L0_rec_W1p, L0_rec_b1p, L0_rec_W2p, L0_rec_b2p)
    return y

_drawn_inputs = setup_inputs


def setup_inputs(seed=0):
    import zlib

    import numpy as np

    out = dict(_drawn_inputs(seed))
    spreads = {'L0_rec_b1a': (0.0, 2.0), 'L0_rec_b1p': (0.0, 0.1)}
    factors = {'L0_rec_W1a': 64.0, 'L0_rec_W2a': 64.0}
    for name, (base, spread) in spreads.items():
        noise = np.random.default_rng([zlib.crc32(name.encode()), seed]).standard_normal(out[name].shape)
        drawn = base * np.exp(spread * noise) if base else spread * noise
        out[name] = jnp.asarray(drawn.astype(out[name].dtype))
    for name, factor in factors.items():
        out[name] = (out[name] * factor).astype(out[name].dtype)
    return out
```

```python
from contextlib import ExitStack

import concourse.bass as bass
from concourse import mybir

F32 = mybir.dt.float32
I32 = mybir.dt.int32
U32 = mybir.dt.uint32
ALU = mybir.AluOpType
ACT = mybir.ActivationFunctionType
AX = mybir.AxisListType

P = 128
CHUNK = 8
HALF = 4
RING = 5
BLOCK = RING * CHUNK
NEG_MASK = -3e38
NEG_START = -1e37


def din_attention(nc, ids, mask, target, emb, w1a, b1a, w2a, b2a, w1p, b1p, w2p, b2p, out):
    B, T = ids.shape
    V, D = emb.shape
    H = w1a.shape[1]
    G = B // P
    N = T // BLOCK
    assert B == G * P and T == N * BLOCK and 2 * D == P and H == P

    with ExitStack() as ctx:
        def sb(name, shape, dt=F32):
            return ctx.enter_context(nc.sbuf_tensor(name, shape, dt))

        def psum(name, shape):
            return ctx.enter_context(nc.psum_tensor(name, shape, F32))

        def sem(name):
            return ctx.enter_context(nc.semaphore(name))

        raw_ids = sb("raw_ids", [P, G, T], I32)
        wrap = sb("wrap", [P, G * T])
        row_idx = sb("row_idx", [P, G * T + BLOCK], U32)
        raw_target = sb("raw_target", [P, G], I32)
        wrap_target = sb("wrap_target", [P, G])
        target_idx = sb("target_idx", [P, G], U32)
        mask_u8 = sb("mask_u8", [P, G, T], mybir.dt.uint8)
        neg_bias = sb("neg_bias", [P, G * T])
        ident = sb("ident", [P, P])
        w_feat = sb("w_feat", [P, H])
        w_diff = sb("w_diff", [D, H])
        w_target = sb("w_target", [D, H])
        wp_feat = sb("wp_feat", [P, H])
        wp_diff = sb("wp_diff", [D, H])
        wp_target = sb("wp_target", [D, H])
        w2a_sb = sb("w2a_sb", [H, 1])
        w2p_sb = sb("w2p_sb", [H, 1])
        b1a_sb = sb("b1a_sb", [H, 1])
        b1p_sb = sb("b1p_sb", [H, 1])
        b2a_sb = sb("b2a_sb", [P, 1])
        b2p_sb = sb("b2p_sb", [1, 1])
        t_rows = sb("t_rows", [P, G, D])
        t_cols = sb("t_cols", [D, G, P])
        c_row = sb("c_row", [H, G, P])

        idx = sb("idx", [P, BLOCK], U32)
        hist = sb("hist", [P, RING, CHUNK + 1, 2, D])
        neg_score = sb("neg_score", [P, RING, CHUNK + 1])
        prob = sb("prob", [P, RING, CHUNK + 1])
        count = sb("count", [P, RING, CHUNK + 1])
        prob_sum = sb("prob_sum", [P, CHUNK + 1])
        weighted = sb("weighted", [P, CHUNK + 1, D])
        feat = sb("feat", [P, 2, HALF, P])
        hidden = sb("hidden", [H, 2, HALF, P])
        relu = sb("relu", [H, 2, HALF, P])

        denom = sb("denom", [P, 1])
        inv = sb("inv", [P, 1])
        user = sb("user", [P, 2, D])
        user_feat = sb("user_feat", [P, P])
        user_relu = sb("user_relu", [H, P])
        logits = sb("logits", [1, B])

        ps_h = psum("ps_h", [P, 2, HALF, P])
        ps_hidden = psum("ps_hidden", [H, 2, HALF, P])
        ps_score = psum("ps_score", [P, 2, 512])
        ps_misc = psum("ps_misc", [P, 512])
        ps_pred = psum("ps_pred", [P, 512])

        ids_in, target_in, mask_in = sem("ids_in"), sem("target_in"), sem("mask_in")
        weights_in, out_stored = sem("weights_in"), sem("out_stored")
        zeroed, ident_ready = sem("zeroed"), sem("ident_ready")
        target_clamp, ids_clamp, mask_step = sem("target_clamp"), sem("ids_clamp"), sem("mask_step")
        target_idx_ready, targets_gathered = sem("target_idx_ready"), sem("targets_gathered")
        weights_folded, targets_transposed = sem("weights_folded"), sem("targets_transposed")
        t_cols_ready, c_row_product = sem("t_cols_ready"), sem("c_row_product")
        c_row_ready, constants_ready, state_reset = sem("c_row_ready"), sem("constants_ready"), sem("state_reset")
        idx_staged, chunk_begun = sem("idx_staged"), sem("chunk_begun")
        gathered = [sem(f"gathered{s}") for s in range(RING)]
        product_ready = sem("product_ready")
        h_transposed, feat_ready, hidden_product = sem("h_transposed"), sem("feat_ready"), sem("hidden_product")
        hidden_ready, relu_ready, scores_ready = sem("hidden_ready"), sem("relu_ready"), sem("scores_ready")
        neg_score_ready, max_ready, probs_ready = sem("neg_score_ready"), sem("max_ready"), sem("probs_ready")
        weighted_ready, sums_ready, denom_ready = sem("weighted_ready"), sem("sums_ready"), sem("denom_ready")
        user_ready, user_transposed, user_feat_ready = sem("user_ready"), sem("user_transposed"), sem("user_feat_ready")
        pred_product, pred_relu_ready, logit_product = sem("pred_product"), sem("pred_relu_ready"), sem("logit_product")
        logits_ready = sem("logits_ready")

        WEIGHT_LOADS = 14
        block = ctx.enter_context(nc.Block())

        @block.sync
        def _(sp):
            sp.dma_start(raw_target[:, :], target).then_inc(target_in, 16)
            sp.dma_start(raw_ids[:, :, :], ids.rearrange("(g p) t -> p g t", p=P)).then_inc(ids_in, 16)
            sp.dma_start(mask_u8[:, :, :], mask.rearrange("(g p) t -> p g t", p=P)).then_inc(mask_in, 16)
            for w1, feat_w, diff_w, target_w in ((w1a, w_feat, w_diff, w_target),
                                                 (w1p, wp_feat, wp_diff, wp_target)):
                sp.dma_start(feat_w[0:D, :], w1[0:D, :]).then_inc(weights_in, 16)
                sp.dma_start(target_w[:, :], w1[D:2 * D, :]).then_inc(weights_in, 16)
                sp.dma_start(diff_w[:, :], w1[2 * D:3 * D, :]).then_inc(weights_in, 16)
                sp.dma_start(feat_w[D:2 * D, :], w1[3 * D:4 * D, :]).then_inc(weights_in, 16)
            sp.dma_start(w2a_sb[:, :], w2a).then_inc(weights_in, 16)
            sp.dma_start(w2p_sb[:, :], w2p).then_inc(weights_in, 16)
            sp.dma_start(b1a_sb[:, :], b1a.rearrange("(h a) -> h a", a=1)).then_inc(weights_in, 16)
            sp.dma_start(b1p_sb[:, :], b1p.rearrange("(h a) -> h a", a=1)).then_inc(weights_in, 16)
            sp.dma_start(b2a_sb[:, :], b2a.rearrange("(h a) -> h a", a=1).broadcast_to([P, 1])).then_inc(weights_in, 16)
            sp.dma_start(b2p_sb[:, :], b2p.rearrange("(h a) -> h a", a=1)).then_inc(weights_in, 16)
            sp.wait_ge(logits_ready, G)
            sp.dma_start(out.rearrange("(a b) -> a b", a=1), logits[:, :]).then_inc(out_stored, 16)
            sp.wait_ge(out_stored, 16)

        @block.gpsimd
        def _(pool):
            nc.gpsimd.memset(ident[:, :], 0.0).then_inc(zeroed, 1)
            pool.wait_ge(zeroed, 1)
            nc.gpsimd.affine_select(out=ident[:, :], in_=ident[:, :], compare_op=ALU.not_equal, fill=1.0,
                                    base=0, pattern=[[-1, P]], channel_multiplier=1).then_inc(ident_ready, 1)
            pool.wait_ge(target_idx_ready, 1)
            for g in range(G):
                pool.indirect_dma_start(t_rows[:, g, :], None, emb,
                                        bass.IndirectOffsetOnAxis(target_idx[:, g:g + 1], 0)
                                        ).then_inc(targets_gathered, 16)
            with pool.Fori(0, G * N) as n:
                for s in range(RING):
                    pool.wait_ge(idx_staged, n * RING + (s + 1))
                    pool.sem_inc(chunk_begun)
                    for j in range(CHUNK):
                        col = s * CHUNK + j
                        pool.indirect_dma_start(hist[:, s, j, 0, :], None, emb,
                                                bass.IndirectOffsetOnAxis(idx[:, col:col + 1], 0)
                                                ).then_inc(gathered[s], 16)

        @block.tensor
        def _(pe):
            pe.wait_ge(ident_ready, 1)
            pe.wait_ge(targets_gathered, 16 * G)
            for g in range(G):
                last = nc.tensor.transpose(ps_misc[0:D, g * P:(g + 1) * P], t_rows[:, g, :], ident[:, :])
            last.then_inc(targets_transposed, 1)
            pe.wait_ge(weights_folded, 4)
            pe.wait_ge(t_cols_ready, 1)
            nc.tensor.matmul(ps_pred[:, :], w_target[:, :], t_cols[:, :, :].rearrange("d g p -> d (g p)"),
                             start=True, stop=True).then_inc(c_row_product, 1)
            pe.wait_ge(c_row_ready, 1)

            with pe.Fori(0, G) as g:
                with pe.Fori(0, N) as i:
                    n = g * N + i
                    first = n * (2 * RING)
                    for step in range(2 * RING + 2):
                        if 1 <= step <= 2 * RING:
                            half = (step - 1) % 2
                            pe.wait_ge(feat_ready, first + step)
                            if step >= 3:
                                pe.wait_ge(hidden_ready, first + (step - 2))
                            nc.tensor.matmul(ps_hidden[:, half, :, :].rearrange("h a b -> h (a b)"), w_feat[:, :],
                                             feat[:, half, :, :].rearrange("f a b -> f (a b)"),
                                             start=True, stop=True).then_inc(hidden_product, 1)
                        if step >= 2:
                            s, half = (step - 2) // 2, step % 2
                            pe.wait_ge(relu_ready, first + (step - 1))
                            if half == 0 and s >= 1:
                                pe.wait_ge(neg_score_ready, n * RING + s)
                            for j in range(HALF):
                                col = s * CHUNK + half * HALF + j
                                last = nc.tensor.matmul(ps_score[:, s % 2, col:col + 1], relu[:, half, j, :],
                                                        w2a_sb[:, :], start=True, stop=True)
                            last.then_inc(scores_ready, 1)
                        if step < 2 * RING:
                            s, half = step // 2, step % 2
                            if half == 0:
                                pe.wait_ge(gathered[s], (n + 1) * (16 * CHUNK))
                                pe.wait_ge(product_ready, n * RING + (s + 1))
                            if step >= 2:
                                pe.wait_ge(feat_ready, first + (step - 1))
                            for j in range(HALF):
                                last = nc.tensor.transpose(
                                    ps_h[:, half, j, :],
                                    hist[:, s, half * HALF + j, :, :].rearrange("p a d -> p (a d)"), ident[:, :])
                            last.then_inc(h_transposed, 1)

                pe.wait_ge(user_ready, (g + 1) * 2)
                nc.tensor.transpose(ps_misc[:, 0:P], user[:, :, :].rearrange("p a d -> p (a d)"), ident[:, :]
                                    ).then_inc(user_transposed, 1)
                nc.tensor.matmul(ps_pred[:, 0:P], wp_target[:, :],
                                 t_cols[:, bass.ds(g, 1), :].rearrange("d a p -> d (a p)"), start=True, stop=False)
                pe.wait_ge(user_feat_ready, g + 1)
                nc.tensor.matmul(ps_pred[:, 0:P], wp_feat[:, :], user_feat[:, :],
                                 start=False, stop=True).then_inc(pred_product, 1)
                pe.wait_ge(pred_relu_ready, g + 1)
                nc.tensor.matmul(ps_misc[0:1, P:2 * P], w2p_sb[:, :], user_relu[:, :],
                                 start=True, stop=True).then_inc(logit_product, 1)

        @block.scalar
        def _(act):
            act.wait_ge(c_row_product, 1)
            act.wait_ge(weights_in, 16 * WEIGHT_LOADS)
            nc.scalar.activation(c_row[:, :, :].rearrange("h g p -> h (g p)"), ps_pred[:, :], ACT.Identity,
                                 bias=b1a_sb[:, 0:1]).then_inc(c_row_ready, 1)

            with act.Fori(0, G) as g:
                with act.Fori(0, N) as i:
                    n = g * N + i
                    first = n * (2 * RING)

                    def relus(q):
                        act.wait_ge(hidden_ready, first + (q + 1))
                        if q >= 2:
                            act.wait_ge(scores_ready, first + (q - 1))
                        nc.scalar.activation(relu[:, q % 2, :, :], hidden[:, q % 2, :, :], ACT.Relu
                                             ).then_inc(relu_ready, 1)

                    def probs(s):
                        act.wait_ge(max_ready, n * RING + (s + 1))
                        nc.scalar.activation(prob[:, s, :], neg_score[:, s, :], ACT.Exp, scale=-1.0,
                                             bias=neg_score[:, (s + 1) % RING, CHUNK:CHUNK + 1]
                                             ).then_inc(probs_ready, 1)

                    def features(q):
                        act.wait_ge(h_transposed, first + (q + 1))
                        if q >= 2:
                            act.wait_ge(hidden_product, first + (q - 1))
                        nc.scalar.copy(feat[:, q % 2, :, :], ps_h[:, q % 2, :, :]).then_inc(feat_ready, 1)

                    for step in range(2 * RING + 2):
                        if 1 <= step <= 2 * RING:
                            relus(step - 1)
                        if step < 2 * RING:
                            features(step)
                        if step >= 3 and step % 2 == 1:
                            probs((step - 3) // 2)

                act.wait_ge(user_transposed, g + 1)
                nc.scalar.copy(user_feat[:, :], ps_misc[:, 0:P]).then_inc(user_feat_ready, 1)
                act.wait_ge(pred_product, g + 1)
                nc.scalar.activation(user_relu[:, :], ps_pred[:, 0:P], ACT.Relu,
                                     bias=b1p_sb[:, 0:1]).then_inc(pred_relu_ready, 1)
                act.wait_ge(logit_product, g + 1)
                nc.scalar.activation(logits[0:1, bass.ds(g * P, P)], ps_misc[0:1, P:2 * P], ACT.Identity,
                                     bias=b2p_sb[0:1, 0:1]).then_inc(logits_ready, 1)

        @block.vector
        def _(dve):
            def clamp(raw, wrapped, done, steps, before):
                nc.vector.tensor_scalar(wrapped, raw, 0, V, ALU.is_lt, ALU.mult).then_inc(steps, 1)
                dve.wait_ge(steps, before + 1)
                nc.vector.tensor_tensor(wrapped, wrapped, raw, ALU.add).then_inc(steps, 1)
                dve.wait_ge(steps, before + 2)
                return nc.vector.tensor_scalar(done, wrapped, 0, V - 1, ALU.max, ALU.min)

            dve.wait_ge(target_in, 16)
            clamp(raw_target[:, :], wrap_target[:, :], target_idx[:, :], target_clamp, 0
                  ).then_inc(target_idx_ready, 1)
            dve.wait_ge(ids_in, 16)
            flat_ids = raw_ids[:, :, :].rearrange("p g t -> p (g t)")
            clamp(flat_ids[:, 0:BLOCK], wrap[:, 0:BLOCK], row_idx[:, 0:BLOCK], ids_clamp, 0).then_inc(ids_clamp, 1)
            dve.wait_ge(ids_clamp, 3)
            nc.vector.tensor_copy(idx[:, :], row_idx[:, 0:BLOCK]).then_inc(idx_staged, RING)
            clamp(flat_ids[:, BLOCK:], wrap[:, BLOCK:], row_idx[:, BLOCK:G * T], ids_clamp, 3).then_inc(ids_clamp, 1)
            nc.vector.memset(row_idx[:, G * T:], 0).then_inc(ids_clamp, 1)
            dve.wait_ge(ids_clamp, 7)
            dve.wait_ge(weights_in, 16 * WEIGHT_LOADS)
            for feat_w, diff_w, target_w in ((w_feat, w_diff, w_target), (wp_feat, wp_diff, wp_target)):
                nc.vector.tensor_tensor(feat_w[0:D, :], feat_w[0:D, :], diff_w[:, :], ALU.add
                                        ).then_inc(weights_folded, 1)
                nc.vector.tensor_tensor(target_w[:, :], target_w[:, :], diff_w[:, :], ALU.subtract
                                        ).then_inc(weights_folded, 1)
            dve.wait_ge(mask_in, 16)
            nc.vector.tensor_scalar(neg_bias[:, :], mask_u8[:, :, :].rearrange("p g t -> p (g t)"),
                                    NEG_MASK, -NEG_MASK, ALU.mult, ALU.add).then_inc(mask_step, 1)
            dve.wait_ge(mask_step, 1)
            nc.vector.tensor_scalar(neg_bias[:, :], neg_bias[:, :], b2a_sb[:, 0:1], None, ALU.subtract
                                    ).then_inc(mask_step, 1)
            dve.wait_ge(mask_step, 2)
            nc.vector.memset(count[:, :, :], 1.0).then_inc(constants_ready, 1)
            dve.wait_ge(targets_transposed, 1)
            nc.vector.tensor_copy(t_cols[:, :, :].rearrange("d g p -> d (g p)"), ps_misc[0:D, :]
                                  ).then_inc(t_cols_ready, 1)
            dve.wait_ge(constants_ready, 1)
            dve.wait_ge(c_row_ready, 1)

            with dve.Fori(0, G) as g:
                nc.vector.memset(hist[:, 0, CHUNK, 0, :], 0.0).then_inc(state_reset, 1)
                nc.vector.memset(count[:, 0, CHUNK:CHUNK + 1], 0.0).then_inc(state_reset, 1)
                nc.vector.memset(neg_score[:, 0, CHUNK:CHUNK + 1], -NEG_START).then_inc(state_reset, 1)

                with dve.Fori(0, N) as i:
                    n = g * N + i
                    first = n * (2 * RING)
                    chunks = n * RING

                    def products(s):
                        dve.wait_ge(gathered[s], (n + 1) * (16 * CHUNK))
                        nc.vector.tensor_tensor(hist[:, s, 0:CHUNK, 1, :], hist[:, s, 0:CHUNK, 0, :],
                                                t_rows[:, bass.ds(g, 1), :].broadcast_to([P, CHUNK, D]),
                                                ALU.mult).then_inc(product_ready, 1)

                    def hidden_sum(q):
                        dve.wait_ge(hidden_product, first + (q + 1))
                        if q >= 2:
                            dve.wait_ge(relu_ready, first + (q - 1))
                        nc.vector.tensor_tensor(hidden[:, q % 2, :, :], ps_hidden[:, q % 2, :, :],
                                                c_row[:, bass.ds(g, 1), :].broadcast_to([H, HALF, P]), ALU.add).then_inc(hidden_ready, 1)

                    def maximum(s):
                        if s == 0:
                            dve.wait_ge(state_reset, (g + 1) * 3)
                        dve.wait_ge(scores_ready, first + (2 * s + 2))
                        nc.vector.scalar_tensor_tensor(
                            out=neg_score[:, s, 0:CHUNK], in0=ps_score[:, s % 2, s * CHUNK:(s + 1) * CHUNK],
                            scalar=-1.0, in1=neg_bias[:, bass.ds(n * BLOCK + s * CHUNK, CHUNK)],
                            op0=ALU.mult, op1=ALU.add).then_inc(neg_score_ready, 1)
                        dve.wait_ge(neg_score_ready, chunks + (s + 1))
                        nc.vector.tensor_reduce(neg_score[:, (s + 1) % RING, CHUNK:CHUNK + 1], neg_score[:, s, :],
                                                AX.X, ALU.min).then_inc(max_ready, 1)

                    def running_sums(s):
                        dve.wait_ge(probs_ready, chunks + (s + 1))
                        nc.vector.tensor_tensor(weighted[:, :, :], hist[:, s, :, 0, :],
                                                prob[:, s, :].unsqueeze(2).broadcast_to([P, CHUNK + 1, D]), ALU.mult
                                                ).then_inc(weighted_ready, 1)
                        nc.vector.tensor_tensor_reduce(
                            out=prob_sum[:, :], in0=prob[:, s, :], in1=count[:, s, :], scale=1.0, scalar=0.0,
                            op0=ALU.mult, op1=ALU.add,
                            accum_out=count[:, (s + 1) % RING, CHUNK:CHUNK + 1]).then_inc(sums_ready, 1)
                        dve.wait_ge(weighted_ready, chunks + (s + 1))
                        nc.vector.tensor_reduce(hist[:, (s + 1) % RING, CHUNK, 0, :],
                                                weighted[:, :, :].rearrange("p j d -> p d j"),
                                                AX.X, ALU.add).then_inc(sums_ready, 1)
                        nc.vector.tensor_copy(idx[:, s * CHUNK:(s + 1) * CHUNK],
                                              row_idx[:, bass.ds((n + 1) * BLOCK + s * CHUNK, CHUNK)]
                                              ).then_inc(idx_staged, 1)
                        dve.wait_ge(sums_ready, (chunks + (s + 1)) * 2)

                    for step in range(2 * RING + 2):
                        if step < 2 * RING and step % 2 == 0:
                            products(step // 2)
                        if 1 <= step <= 2 * RING:
                            hidden_sum(step - 1)
                        if step >= 3 and step % 2 == 1:
                            maximum((step - 3) // 2)
                            running_sums((step - 3) // 2)

                nc.vector.tensor_scalar(denom[:, :], count[:, 0, CHUNK:CHUNK + 1], 1e-8, None, ALU.max
                                        ).then_inc(denom_ready, 1)
                dve.wait_ge(denom_ready, g * 2 + 1)
                nc.vector.reciprocal(inv[:, :], denom[:, :]).then_inc(denom_ready, 1)
                dve.wait_ge(denom_ready, g * 2 + 2)
                nc.vector.tensor_scalar(user[:, 0, :], hist[:, 0, CHUNK, 0, :], inv[:, 0:1], None, ALU.mult
                                        ).then_inc(user_ready, 1)
                dve.wait_ge(user_ready, g * 2 + 1)
                nc.vector.tensor_tensor(user[:, 1, :], user[:, 0, :],
                                        t_rows[:, bass.ds(g, 1), :].rearrange("p a d -> p (a d)"), ALU.mult
                                        ).then_inc(user_ready, 1)


def kernel(**inputs):
    import numpy as np
    import concourse.bacc as bacc
    from concourse import mybir as mb
    from concourse.bass_utils import run_bass_kernel_spmd

    nc = bacc.Bacc("TRN2", target_bir_lowering=False, num_devices=1)
    order = ["r_history_ids", "r_history_mask", "r_target_ids", "L0_rec_emb", "L0_rec_W1a", "L0_rec_b1a",
             "L0_rec_W2a", "L0_rec_b2a", "L0_rec_W1p", "L0_rec_b1p", "L0_rec_W2p", "L0_rec_b2p"]
    arrays, args = {}, []
    for name in order:
        a = np.ascontiguousarray(inputs[name])
        if name == "r_target_ids":
            a = np.ascontiguousarray(a.reshape(-1, P).T)
        arrays[name] = a
        args.append(nc.dram_tensor(name, a.shape, mb.dt.from_np(a.dtype), kind="ExternalInput").ap())
    out = nc.dram_tensor("logits_out", (inputs["r_target_ids"].shape[0],), mb.dt.float32,
                         kind="ExternalOutput").ap()
    din_attention(nc, *args, out)
    r = run_bass_kernel_spmd(nc, [arrays], core_ids=[0])
    return r.results[0]["logits_out"]
```

```python
from contextlib import ExitStack

import concourse.bass as bass
from concourse import mybir

F32 = mybir.dt.float32
I32 = mybir.dt.int32
U32 = mybir.dt.uint32
ALU = mybir.AluOpType
ACT = mybir.ActivationFunctionType
AX = mybir.AxisListType

P = 128
CHUNK = 8
HALF = 4
RING = 5
BLOCK = RING * CHUNK
NEG_MASK = -3e38
NEG_START = -1e37


def din_attention(nc, ids, mask, target, emb, w1a, b1a, w2a, b2a, w1p, b1p, w2p, b2p, out):
    B, T = ids.shape
    V, D = emb.shape
    H = w1a.shape[1]
    G = B // P
    N = T // BLOCK
    K = G * N
    assert B == G * P and T == N * BLOCK and 2 * D == P and H == P

    with ExitStack() as ctx:
        def sb(name, shape, dt=F32):
            return ctx.enter_context(nc.sbuf_tensor(name, shape, dt))

        def psum(name, shape):
            return ctx.enter_context(nc.psum_tensor(name, shape, F32))

        def sem(name):
            return ctx.enter_context(nc.semaphore(name))

        raw_ids = sb("raw_ids", [P, G, T], I32)
        keys = sb("keys", [P, G, T])
        raw_target = sb("raw_target", [P, G], I32)
        wrap_target = sb("wrap_target", [P, G])
        target_idx = sb("target_idx", [P, G], U32)
        mask_u8 = sb("mask_u8", [P, G, T], mybir.dt.uint8)
        left = sb("left", [P, T])
        is_last = sb("is_last", [P, T])
        top = sb("top", [P, CHUNK])
        top_is_last = sb("top_is_last", [P, CHUNK])
        copies_left = sb("copies_left", [P, 1])
        copies_top = sb("copies_top", [P, 1])
        neg_key = sb("neg_key", [P, CHUNK])
        list_key = sb("list_key", [P, K * BLOCK])
        list_more = sb("list_more", [P, K * RING])
        row_idx = sb("row_idx", [P, (K + 1) * BLOCK], U32)
        multiplicity = sb("multiplicity", [P, K * BLOCK])
        neg_bias = sb("neg_bias", [P, K * BLOCK])
        most_left = sb("most_left", [P, 1])
        ones = sb("ones", [P, 1])
        more_left = sb("more_left", [1, 1], I32)
        saved_sum = sb("saved_sum", [P, G, D])
        saved_count = sb("saved_count", [P, G])
        saved_neg_max = sb("saved_neg_max", [P, G])
        ident = sb("ident", [P, P])
        w_feat = sb("w_feat", [P, H])
        w_diff = sb("w_diff", [D, H])
        w_target = sb("w_target", [D, H])
        wp_feat = sb("wp_feat", [P, H])
        wp_diff = sb("wp_diff", [D, H])
        wp_target = sb("wp_target", [D, H])
        w2a_row = sb("w2a_row", [P, H])
        w2p_sb = sb("w2p_sb", [H, 1])
        b1a_row = sb("b1a_row", [P, H])
        b1p_sb = sb("b1p_sb", [H, 1])
        b2a_sb = sb("b2a_sb", [P, 1])
        b2p_sb = sb("b2p_sb", [1, 1])
        t_rows = sb("t_rows", [P, G, D])
        t_cols = sb("t_cols", [D, G, P])
        c_row = sb("c_row", [P, G, H])

        idx = sb("idx", [P, BLOCK], U32)
        hist = sb("hist", [P, RING, CHUNK + 1, 2, D])
        neg_score = sb("neg_score", [P, RING, CHUNK + 1])
        prob = sb("prob", [P, RING, CHUNK + 1])
        count = sb("count", [P, RING, CHUNK + 1])
        prob_sum = sb("prob_sum", [P, CHUNK + 1])
        weighted = sb("weighted", [P, CHUNK + 1, D])
        feat = sb("feat", [P, 2, HALF, P])
        hidden = sb("hidden", [P, 2, HALF, H])
        relu_w2 = sb("relu_w2", [P, CHUNK, H])
        neg_dot = sb("neg_dot", [P, RING, CHUNK])

        denom = sb("denom", [P, 1])
        inv = sb("inv", [P, 1])
        user = sb("user", [P, 2, D])
        user_feat = sb("user_feat", [P, P])
        user_relu = sb("user_relu", [H, P])
        logits = sb("logits", [1, B])

        ps_h = psum("ps_h", [P, 2, HALF, P])
        ps_hidden = psum("ps_hidden", [P, 2, HALF, H])
        ps_misc = psum("ps_misc", [P, 512])
        ps_pred = psum("ps_pred", [P, 512])

        keys_step, keys_copied = sem("keys_step"), sem("keys_copied")
        top_ready, removed, round_parts = sem("top_ready"), sem("removed"), sem("round_parts")
        listed, lists_step, keys_kept = sem("listed"), sem("lists_step"), sem("keys_kept")
        left_max, left_sum, more_left_ready = sem("left_max"), sem("left_sum"), sem("more_left_ready")
        rest_staged, prob_counted, state_saved = sem("rest_staged"), sem("prob_counted"), sem("state_saved")
        ids_in, target_in, mask_in = sem("ids_in"), sem("target_in"), sem("mask_in")
        weights_in, out_stored = sem("weights_in"), sem("out_stored")
        zeroed, ident_ready = sem("zeroed"), sem("ident_ready")
        target_clamp = sem("target_clamp")
        target_idx_ready, targets_gathered = sem("target_idx_ready"), sem("targets_gathered")
        weights_folded, targets_transposed = sem("weights_folded"), sem("targets_transposed")
        t_cols_ready, c_row_product = sem("t_cols_ready"), sem("c_row_product")
        c_row_ready, constants_ready, state_loaded = sem("c_row_ready"), sem("constants_ready"), sem("state_loaded")
        waited = sem("waited")
        idx_staged = sem("idx_staged")
        gathered = [sem(f"gathered{s}") for s in range(RING)]
        product_ready = sem("product_ready")
        h_transposed, feat_ready, hidden_product = sem("h_transposed"), sem("feat_ready"), sem("hidden_product")
        hidden_ready, dots_ready, w2a_negated = sem("hidden_ready"), sem("dots_ready"), sem("w2a_negated")
        neg_score_ready, max_ready, probs_ready = sem("neg_score_ready"), sem("max_ready"), sem("probs_ready")
        weighted_ready, sums_ready, denom_ready = sem("weighted_ready"), sem("sums_ready"), sem("denom_ready")
        user_ready, user_transposed, user_feat_ready = sem("user_ready"), sem("user_transposed"), sem("user_feat_ready")
        pred_product, pred_relu_ready, logit_product = sem("pred_product"), sem("pred_relu_ready"), sem("logit_product")
        logits_ready = sem("logits_ready")

        WEIGHT_LOADS = 14
        block = ctx.enter_context(nc.Block())

        def needs_rest(engine):
            return engine.value_load(more_left[0:1, 0:1], min_val=0, max_val=1) != 0

        @block.sync
        def _(sp):
            sp.dma_start(raw_target[:, :], target).then_inc(target_in, 16)
            sp.dma_start(raw_ids[:, :, :], ids.rearrange("(g p) t -> p g t", p=P)).then_inc(ids_in, 16)
            sp.dma_start(mask_u8[:, :, :], mask.rearrange("(g p) t -> p g t", p=P)).then_inc(mask_in, 16)
            for w1, feat_w, diff_w, target_w in ((w1a, w_feat, w_diff, w_target),
                                                 (w1p, wp_feat, wp_diff, wp_target)):
                sp.dma_start(feat_w[0:D, :], w1[0:D, :]).then_inc(weights_in, 16)
                sp.dma_start(target_w[:, :], w1[D:2 * D, :]).then_inc(weights_in, 16)
                sp.dma_start(diff_w[:, :], w1[2 * D:3 * D, :]).then_inc(weights_in, 16)
                sp.dma_start(feat_w[D:2 * D, :], w1[3 * D:4 * D, :]).then_inc(weights_in, 16)
            sp.dma_start(w2a_row[:, :], w2a.rearrange("h a -> a h").broadcast_to([P, H])).then_inc(weights_in, 16)
            sp.dma_start(w2p_sb[:, :], w2p).then_inc(weights_in, 16)
            sp.dma_start(b1a_row[:, :], b1a.rearrange("(a h) -> a h", a=1).broadcast_to([P, H])
                         ).then_inc(weights_in, 16)
            sp.dma_start(b1p_sb[:, :], b1p.rearrange("(h a) -> h a", a=1)).then_inc(weights_in, 16)
            sp.dma_start(b2a_sb[:, :], b2a.rearrange("(h a) -> h a", a=1).broadcast_to([P, 1])).then_inc(weights_in, 16)
            sp.dma_start(b2p_sb[:, :], b2p.rearrange("(h a) -> h a", a=1)).then_inc(weights_in, 16)
            sp.wait_ge(logits_ready, G)
            sp.wait_ge(more_left_ready, 1)
            with sp.If(needs_rest(sp)):
                sp.wait_ge(logits_ready, K)
            sp.dma_start(out.rearrange("(a b) -> a b", a=1), logits[:, :]).then_inc(out_stored, 16)
            sp.wait_ge(out_stored, 16)

        @block.gpsimd
        def _(pool):
            nc.gpsimd.memset(ones[:, :], 1.0).then_inc(ident_ready, 1)
            nc.gpsimd.memset(ident[:, :], 0.0).then_inc(zeroed, 1)
            pool.wait_ge(zeroed, 1)
            nc.gpsimd.affine_select(out=ident[:, :], in_=ident[:, :], compare_op=ALU.not_equal, fill=1.0,
                                    base=0, pattern=[[-1, P]], channel_multiplier=1).then_inc(ident_ready, 1)
            pool.wait_ge(target_idx_ready, 1)
            for g in range(G):
                pool.indirect_dma_start(t_rows[:, g, :], None, emb,
                                        bass.IndirectOffsetOnAxis(target_idx[:, g:g + 1], 0)
                                        ).then_inc(targets_gathered, 16)
            def gathers(k):
                for s in range(RING):
                    pool.wait_ge(idx_staged, k * RING + (s + 1))
                    pool.sem_inc(waited)
                    for j in range(CHUNK):
                        col = s * CHUNK + j
                        pool.indirect_dma_start(hist[:, s, j, 0, :], None, emb,
                                                bass.IndirectOffsetOnAxis(idx[:, col:col + 1], 0)
                                                ).then_inc(gathered[s], 16)

            with pool.Fori(0, G) as k:
                gathers(k)
            pool.wait_ge(more_left_ready, 1)
            with pool.If(needs_rest(pool)):
                pool.wait_ge(rest_staged, 1)
                with pool.Fori(G, K) as k:
                    gathers(k)

        @block.tensor
        def _(pe):
            pe.wait_ge(ident_ready, 2)
            pe.wait_ge(targets_gathered, 16 * G)
            for g in range(G):
                last = nc.tensor.transpose(ps_misc[0:D, g * P:(g + 1) * P], t_rows[:, g, :], ident[:, :])
            last.then_inc(targets_transposed, 1)
            pe.wait_ge(weights_folded, 4)
            pe.wait_ge(t_cols_ready, 1)
            for g in range(G):
                last = nc.tensor.matmul(ps_pred[:, g * H:(g + 1) * H], t_cols[:, g, :], w_target[:, :],
                                        start=True, stop=True)
            last.then_inc(c_row_product, 1)
            pe.wait_ge(t_cols_ready, 1)
            pe.wait_ge(left_max, 1)
            nc.tensor.matmul(ps_misc[0:1, 0:1], most_left[:, :], ones[:, :], start=True, stop=True
                             ).then_inc(left_sum, 1)
            pe.wait_ge(more_left_ready, 1)
            pe.wait_ge(c_row_ready, 1)

            def chunks_of(k, g):
                first = k * (2 * RING)
                for s in range(RING):
                    pe.wait_ge(gathered[s], (k + 1) * (16 * CHUNK))
                    pe.wait_ge(product_ready, k * RING + (s + 1))
                    for half in range(2):
                        q = 2 * s + half
                        if q >= 2:
                            pe.wait_ge(feat_ready, first + (q - 1))
                        for j in range(HALF):
                            last = nc.tensor.transpose(
                                ps_h[:, half, j, :],
                                hist[:, s, half * HALF + j, :, :].rearrange("p a d -> p (a d)"), ident[:, :])
                        last.then_inc(h_transposed, 1)
                    for half in range(2):
                        q = 2 * s + half
                        pe.wait_ge(feat_ready, first + (q + 1))
                        if q >= 2:
                            pe.wait_ge(hidden_ready, first + (q - 1))
                        for j in range(HALF):
                            last = nc.tensor.matmul(ps_hidden[:, half, j, :], feat[:, half, j, :], w_feat[:, :],
                                                    start=True, stop=True)
                        last.then_inc(hidden_product, 1)

                pe.wait_ge(user_ready, (k + 1) * 2)
                nc.tensor.transpose(ps_misc[:, 0:P], user[:, :, :].rearrange("p a d -> p (a d)"), ident[:, :]
                                    ).then_inc(user_transposed, 1)
                nc.tensor.matmul(ps_pred[:, 0:P], wp_target[:, :],
                                 t_cols[:, bass.ds(g, 1), :].rearrange("d a p -> d (a p)"), start=True, stop=False)
                pe.wait_ge(user_feat_ready, k + 1)
                nc.tensor.matmul(ps_pred[:, 0:P], wp_feat[:, :], user_feat[:, :],
                                 start=False, stop=True).then_inc(pred_product, 1)
                pe.wait_ge(pred_relu_ready, k + 1)
                nc.tensor.matmul(ps_misc[0:1, P:2 * P], w2p_sb[:, :], user_relu[:, :],
                                 start=True, stop=True).then_inc(logit_product, 1)

            def rest():
                with pe.Fori(1, N) as i:
                    with pe.Fori(0, G) as g:
                        chunks_of(i * G + g, g)

            with pe.Fori(0, G) as g:
                chunks_of(g, g)
            with pe.If(needs_rest(pe)):
                rest()

        @block.scalar
        def _(act):
            def chunks_of(k, g):
                first = k * (2 * RING)

                def probs(s):
                    act.wait_ge(max_ready, k * RING + (s + 1))
                    nc.scalar.activation(prob[:, s, :], neg_score[:, s, :], ACT.Exp, scale=-1.0,
                                         bias=neg_score[:, (s + 1) % RING, CHUNK:CHUNK + 1]
                                         ).then_inc(probs_ready, 1)

                def features(q):
                    act.wait_ge(h_transposed, first + (q + 1))
                    if q >= 2:
                        act.wait_ge(hidden_product, first + (q - 1))
                    nc.scalar.copy(feat[:, q % 2, :, :], ps_h[:, q % 2, :, :]).then_inc(feat_ready, 1)

                features(0)
                for s in range(RING):
                    features(2 * s + 1)
                    if s + 1 < RING:
                        features(2 * s + 2)
                    probs(s)

                act.wait_ge(user_transposed, k + 1)
                nc.scalar.copy(user_feat[:, :], ps_misc[:, 0:P]).then_inc(user_feat_ready, 1)
                act.wait_ge(pred_product, k + 1)
                nc.scalar.activation(user_relu[:, :], ps_pred[:, 0:P], ACT.Relu,
                                     bias=b1p_sb[:, 0:1]).then_inc(pred_relu_ready, 1)
                act.wait_ge(logit_product, k + 1)
                nc.scalar.activation(logits[0:1, bass.ds(g * P, P)], ps_misc[0:1, P:2 * P], ACT.Identity,
                                     bias=b2p_sb[0:1, 0:1]).then_inc(logits_ready, 1)

            with act.Fori(0, G) as g:
                chunks_of(g, g)
            act.wait_ge(more_left_ready, 1)
            with act.If(needs_rest(act)):
                with act.Fori(1, N) as i:
                    with act.Fori(0, G) as g:
                        chunks_of(i * G + g, g)

        @block.vector
        def _(dve):
            dve.wait_ge(target_in, 16)
            nc.vector.tensor_scalar(wrap_target[:, :], raw_target[:, :], 0, V, ALU.is_lt, ALU.mult
                                    ).then_inc(target_clamp, 1)
            dve.wait_ge(target_clamp, 1)
            nc.vector.tensor_tensor(wrap_target[:, :], wrap_target[:, :], raw_target[:, :], ALU.add
                                    ).then_inc(target_clamp, 1)
            dve.wait_ge(target_clamp, 2)
            nc.vector.tensor_scalar(target_idx[:, :], wrap_target[:, :], 0, V - 1, ALU.max, ALU.min
                                    ).then_inc(target_idx_ready, 1)

            flat_keys = keys[:, :, :].rearrange("p g t -> p (g t)")
            flat_ids = raw_ids[:, :, :].rearrange("p g t -> p (g t)")
            flat_mask = mask_u8[:, :, :].rearrange("p g t -> p (g t)")

            def make_keys(lo, hi, before):
                part = slice(lo * T, hi * T)
                nc.vector.tensor_scalar(flat_keys[:, part], flat_ids[:, part], 0, -V, ALU.is_lt, ALU.mult
                                        ).then_inc(keys_step, 1)
                dve.wait_ge(keys_step, before + 1)
                nc.vector.scalar_tensor_tensor(out=flat_keys[:, part], in0=flat_ids[:, part], scalar=-1.0,
                                               in1=flat_keys[:, part], op0=ALU.mult, op1=ALU.add
                                               ).then_inc(keys_step, 1)
                dve.wait_ge(keys_step, before + 2)
                nc.vector.tensor_scalar(flat_keys[:, part], flat_keys[:, part], 0, -(V - 1), ALU.min, ALU.max
                                        ).then_inc(keys_step, 1)
                dve.wait_ge(keys_step, before + 3)
                nc.vector.scalar_tensor_tensor(out=flat_keys[:, part], in0=flat_keys[:, part], scalar=float(V),
                                               in1=flat_mask[:, part], op0=ALU.add, op1=ALU.mult
                                               ).then_inc(keys_step, 1)
                dve.wait_ge(keys_step, before + 4)

            def one_round(r, chunk):
                nc.vector.max(top[:, :], left[:, :]).then_inc(top_ready, 1)
                dve.wait_ge(top_ready, r + 1)
                last = top[:, CHUNK - 1:CHUNK]
                nc.vector.tensor_scalar(is_last[:, :], left[:, :], last, None, ALU.is_equal, ALU.add,
                                        accum_out=copies_left[:, :]).then_inc(round_parts, 1)
                nc.vector.scalar_tensor_tensor(out=left[:, :], in0=left[:, :], scalar=last, in1=left[:, :],
                                               op0=ALU.is_lt, op1=ALU.mult).then_inc(removed, 1)
                nc.vector.tensor_scalar(top_is_last[:, :], top[:, :], last, None, ALU.is_equal, ALU.add,
                                        accum_out=copies_top[:, :]).then_inc(round_parts, 1)
                nc.vector.tensor_scalar(neg_key[:, :], top[:, :], 1.0, -1.0, ALU.max, ALU.mult
                                        ).then_inc(round_parts, 1)
                nc.vector.tensor_copy(list_key[:, bass.ds(chunk * CHUNK, CHUNK)], top[:, :]).then_inc(listed, 1)
                dve.wait_ge(round_parts, (r + 1) * 3)
                nc.vector.tensor_scalar(row_idx[:, bass.ds(chunk * CHUNK, CHUNK)], neg_key[:, :], float(V), None,
                                        ALU.add).then_inc(listed, 1)
                nc.vector.tensor_tensor(list_more[:, bass.ds(chunk, 1)], copies_left[:, :], copies_top[:, :],
                                        ALU.subtract).then_inc(listed, 1)
                dve.wait_ge(listed, (r + 1) * 3)
                dve.wait_ge(removed, r + 1)
                dve.sem_inc(waited)

            def finish_lists(lo, hi, before):
                cols, heads = slice(lo * BLOCK, hi * BLOCK), slice(lo * RING, hi * RING)
                by_chunk = multiplicity[:, cols].rearrange("p (c j) -> p c j", j=CHUNK)
                nc.vector.tensor_scalar(multiplicity[:, cols], list_key[:, cols], 0.0, None, ALU.is_gt
                                        ).then_inc(lists_step, 1)
                nc.vector.tensor_scalar(neg_bias[:, cols], list_key[:, cols], 0.0, -NEG_MASK,
                                        ALU.is_equal, ALU.mult).then_inc(lists_step, 1)
                dve.wait_ge(lists_step, before + 2)
                nc.vector.scalar_tensor_tensor(out=by_chunk[:, :, CHUNK - 1], in0=list_more[:, heads], scalar=1.0,
                                               in1=by_chunk[:, :, CHUNK - 1], op0=ALU.add, op1=ALU.mult
                                               ).then_inc(lists_step, 1)
                nc.vector.tensor_scalar(neg_bias[:, cols], neg_bias[:, cols], b2a_sb[:, 0:1], None, ALU.subtract
                                        ).then_inc(lists_step, 1)
                dve.wait_ge(lists_step, before + 4)

            dve.wait_ge(ids_in, 16)
            dve.wait_ge(mask_in, 16)
            make_keys(0, 1, 0)
            nc.vector.tensor_copy(left[:, :], keys[:, 0, :]).then_inc(keys_copied, 1)
            dve.wait_ge(keys_copied, 1)
            for s in range(RING):
                one_round(s, s)
                nc.vector.tensor_copy(idx[:, s * CHUNK:(s + 1) * CHUNK], row_idx[:, s * CHUNK:(s + 1) * CHUNK]
                                      ).then_inc(idx_staged, 1)
            nc.vector.tensor_copy(keys[:, 0, :], left[:, :]).then_inc(keys_kept, 1)
            make_keys(1, G, 4)
            with dve.Fori(1, G) as g:
                nc.vector.tensor_copy(left[:, :], keys[:, bass.ds(g, 1), :].rearrange("p a t -> p (a t)")
                                      ).then_inc(keys_copied, 1)
                dve.wait_ge(keys_copied, g + 1)
                dve.sem_inc(waited)
                for s in range(RING):
                    one_round(g * RING + s, g * RING + s)
                nc.vector.tensor_copy(keys[:, bass.ds(g, 1), :].rearrange("p a t -> p (a t)"), left[:, :]
                                      ).then_inc(keys_kept, 1)
                dve.wait_ge(keys_kept, g + 1)
            nc.vector.tensor_reduce(most_left[:, :], flat_keys, AX.X, ALU.max).then_inc(left_max, 1)
            dve.wait_ge(weights_in, 16 * WEIGHT_LOADS)
            for feat_w, diff_w, target_w in ((w_feat, w_diff, w_target), (wp_feat, wp_diff, wp_target)):
                nc.vector.tensor_tensor(feat_w[0:D, :], feat_w[0:D, :], diff_w[:, :], ALU.add
                                        ).then_inc(weights_folded, 1)
                nc.vector.tensor_tensor(target_w[:, :], target_w[:, :], diff_w[:, :], ALU.subtract
                                        ).then_inc(weights_folded, 1)
            nc.vector.tensor_scalar(w2a_row[:, :], w2a_row[:, :], -1.0, None, ALU.mult).then_inc(w2a_negated, 1)
            dve.wait_ge(targets_transposed, 1)
            nc.vector.tensor_copy(t_cols[:, :, :].rearrange("d g p -> d (g p)"), ps_misc[0:D, :]
                                  ).then_inc(t_cols_ready, 1)
            finish_lists(0, G, 0)
            nc.vector.memset(count[:, :, :], 1.0).then_inc(constants_ready, 1)
            nc.vector.memset(saved_sum[:, :, :], 0.0).then_inc(constants_ready, 1)
            nc.vector.memset(saved_count[:, :], 0.0).then_inc(constants_ready, 1)
            nc.vector.memset(saved_neg_max[:, :], -NEG_START).then_inc(constants_ready, 1)
            nc.vector.memset(row_idx[:, G * BLOCK:(G + 1) * BLOCK], 0).then_inc(constants_ready, 1)
            nc.vector.memset(row_idx[:, K * BLOCK:], 0).then_inc(constants_ready, 1)
            dve.wait_ge(constants_ready, 6)
            dve.wait_ge(c_row_product, 1)
            nc.vector.tensor_tensor(c_row[:, :, :], ps_pred[:, :].rearrange("p (g h) -> p g h", g=G),
                                    b1a_row[:, :].unsqueeze(1).broadcast_to([P, G, H]), ALU.add
                                    ).then_inc(c_row_ready, 1)
            dve.wait_ge(left_sum, 1)
            nc.vector.tensor_scalar(more_left[:, :], ps_misc[0:1, 0:1], 0.0, None, ALU.is_gt
                                    ).then_inc(more_left_ready, 1)
            dve.wait_ge(c_row_ready, 1)
            dve.wait_ge(w2a_negated, 1)

            def chunks_of(k, g):
                first, chunks = k * (2 * RING), k * RING
                nc.vector.tensor_copy(hist[:, 0, CHUNK, 0, :], saved_sum[:, bass.ds(g, 1), :].rearrange(
                    "p a d -> p (a d)")).then_inc(state_loaded, 1)
                nc.vector.tensor_copy(count[:, 0, CHUNK:CHUNK + 1], saved_count[:, bass.ds(g, 1)]
                                      ).then_inc(state_loaded, 1)
                nc.vector.tensor_copy(neg_score[:, 0, CHUNK:CHUNK + 1], saved_neg_max[:, bass.ds(g, 1)]
                                      ).then_inc(state_loaded, 1)

                def products(s):
                    dve.wait_ge(gathered[s], (k + 1) * (16 * CHUNK))
                    nc.vector.tensor_tensor(hist[:, s, 0:CHUNK, 1, :], hist[:, s, 0:CHUNK, 0, :],
                                            t_rows[:, bass.ds(g, 1), :].broadcast_to([P, CHUNK, D]),
                                            ALU.mult).then_inc(product_ready, 1)

                def half_scores(q):
                    half, slot = q % 2, q * HALF % CHUNK
                    dve.wait_ge(hidden_product, first + (q + 1))
                    nc.vector.tensor_tensor(hidden[:, half, :, :], ps_hidden[:, half, :, :],
                                            c_row[:, bass.ds(g, 1), :].broadcast_to([P, HALF, H]), ALU.add
                                            ).then_inc(hidden_ready, 1)
                    dve.wait_ge(hidden_ready, first + (q + 1))
                    for j in range(HALF):
                        last = nc.vector.scalar_tensor_tensor(
                            out=relu_w2[:, slot + j, :], in0=hidden[:, half, j, :], scalar=0.0,
                            in1=w2a_row[:, :], op0=ALU.max, op1=ALU.mult,
                            accum_out=neg_dot[:, q // 2, slot + j:slot + j + 1])
                    last.then_inc(dots_ready, 1)

                def maximum(s):
                    if s == 0:
                        dve.wait_ge(state_loaded, (k + 1) * 3)
                    dve.wait_ge(dots_ready, first + (2 * s + 2))
                    nc.vector.tensor_tensor(neg_score[:, s, 0:CHUNK], neg_dot[:, s, :],
                                            neg_bias[:, bass.ds(k * BLOCK + s * CHUNK, CHUNK)], ALU.add
                                            ).then_inc(neg_score_ready, 1)
                    dve.wait_ge(neg_score_ready, chunks + (s + 1))
                    nc.vector.tensor_reduce(neg_score[:, (s + 1) % RING, CHUNK:CHUNK + 1], neg_score[:, s, :],
                                            AX.X, ALU.min).then_inc(max_ready, 1)

                def running_sums(s):
                    dve.wait_ge(probs_ready, chunks + (s + 1))
                    nc.vector.tensor_tensor(prob[:, s, 0:CHUNK], prob[:, s, 0:CHUNK],
                                            multiplicity[:, bass.ds(k * BLOCK + s * CHUNK, CHUNK)], ALU.mult
                                            ).then_inc(prob_counted, 1)
                    dve.wait_ge(prob_counted, chunks + (s + 1))
                    nc.vector.tensor_tensor(weighted[:, :, :], hist[:, s, :, 0, :],
                                            prob[:, s, :].unsqueeze(2).broadcast_to([P, CHUNK + 1, D]), ALU.mult
                                            ).then_inc(weighted_ready, 1)
                    nc.vector.tensor_tensor_reduce(
                        out=prob_sum[:, :], in0=prob[:, s, :], in1=count[:, s, :], scale=1.0, scalar=0.0,
                        op0=ALU.mult, op1=ALU.add,
                        accum_out=count[:, (s + 1) % RING, CHUNK:CHUNK + 1]).then_inc(sums_ready, 1)
                    dve.wait_ge(weighted_ready, chunks + (s + 1))
                    nc.vector.tensor_reduce(hist[:, (s + 1) % RING, CHUNK, 0, :],
                                            weighted[:, :, :].rearrange("p j d -> p d j"),
                                            AX.X, ALU.add).then_inc(sums_ready, 1)
                    nc.vector.tensor_copy(idx[:, s * CHUNK:(s + 1) * CHUNK],
                                          row_idx[:, bass.ds((k + 1) * BLOCK + s * CHUNK, CHUNK)]
                                          ).then_inc(idx_staged, 1)
                    dve.wait_ge(sums_ready, (chunks + (s + 1)) * 2)

                products(0)
                for s in range(RING):
                    half_scores(2 * s)
                    if s + 1 < RING:
                        products(s + 1)
                    half_scores(2 * s + 1)
                    maximum(s)
                    running_sums(s)

                nc.vector.tensor_scalar(denom[:, :], count[:, 0, CHUNK:CHUNK + 1], 1e-8, None, ALU.max
                                        ).then_inc(denom_ready, 1)
                dve.wait_ge(denom_ready, k * 2 + 1)
                nc.vector.reciprocal(inv[:, :], denom[:, :]).then_inc(denom_ready, 1)
                dve.wait_ge(denom_ready, k * 2 + 2)
                nc.vector.tensor_scalar(user[:, 0, :], hist[:, 0, CHUNK, 0, :], inv[:, 0:1], None, ALU.mult
                                        ).then_inc(user_ready, 1)
                dve.wait_ge(user_ready, k * 2 + 1)
                nc.vector.tensor_tensor(user[:, 1, :], user[:, 0, :],
                                        t_rows[:, bass.ds(g, 1), :].rearrange("p a d -> p (a d)"), ALU.mult
                                        ).then_inc(user_ready, 1)

                nc.vector.tensor_copy(saved_sum[:, bass.ds(g, 1), :].rearrange("p a d -> p (a d)"),
                                      hist[:, 0, CHUNK, 0, :]).then_inc(state_saved, 1)
                nc.vector.tensor_copy(saved_count[:, bass.ds(g, 1)], count[:, 0, CHUNK:CHUNK + 1]
                                      ).then_inc(state_saved, 1)
                nc.vector.tensor_copy(saved_neg_max[:, bass.ds(g, 1)], neg_score[:, 0, CHUNK:CHUNK + 1]
                                      ).then_inc(state_saved, 1)
                dve.wait_ge(state_saved, (k + 1) * 3)

            with dve.Fori(0, G) as g:
                chunks_of(g, g)
            dve.wait_ge(more_left_ready, 1)
            with dve.If(needs_rest(dve)):
                with dve.Fori(0, G) as g:
                    nc.vector.tensor_copy(left[:, :], keys[:, bass.ds(g, 1), :].rearrange("p a t -> p (a t)")
                                          ).then_inc(keys_copied, 1)
                    dve.wait_ge(keys_copied, g + (G + 1))
                    dve.sem_inc(waited)
                    with dve.Fori(1, N) as i:
                        done = G * RING + g * ((N - 1) * RING) + (i - 1) * RING
                        for s in range(RING):
                            one_round(done + s, (i * G + g) * RING + s)
                finish_lists(G, K, 4)
                nc.vector.tensor_copy(idx[:, :], row_idx[:, G * BLOCK:(G + 1) * BLOCK]).then_inc(rest_staged, 1)
                with dve.Fori(1, N) as i:
                    with dve.Fori(0, G) as g:
                        chunks_of(i * G + g, g)


def kernel(**inputs):
    import numpy as np
    import concourse.bacc as bacc
    from concourse import mybir as mb
    from concourse.bass_utils import run_bass_kernel_spmd

    nc = bacc.Bacc("TRN2", target_bir_lowering=False, num_devices=1)
    order = ["r_history_ids", "r_history_mask", "r_target_ids", "L0_rec_emb", "L0_rec_W1a", "L0_rec_b1a",
             "L0_rec_W2a", "L0_rec_b2a", "L0_rec_W1p", "L0_rec_b1p", "L0_rec_W2p", "L0_rec_b2p"]
    arrays, args = {}, []
    for name in order:
        a = np.ascontiguousarray(inputs[name])
        if name == "r_target_ids":
            a = np.ascontiguousarray(a.reshape(-1, P).T)
        arrays[name] = a
        args.append(nc.dram_tensor(name, a.shape, mb.dt.from_np(a.dtype), kind="ExternalInput").ap())
    out = nc.dram_tensor("logits_out", (inputs["r_target_ids"].shape[0],), mb.dt.float32,
                         kind="ExternalOutput").ap()
    din_attention(nc, *args, out)
    r = run_bass_kernel_spmd(nc, [arrays], core_ids=[0])
    return r.results[0]["logits_out"]
```

```python
from contextlib import ExitStack

import concourse.bass as bass
from concourse import mybir

F32 = mybir.dt.float32
I32 = mybir.dt.int32
U32 = mybir.dt.uint32
ALU = mybir.AluOpType
ACT = mybir.ActivationFunctionType
AX = mybir.AxisListType

P = 128
CHUNK = 8
HALF = 4
RING = 4
BLOCK = RING * CHUNK
NEG_MASK = -3e38
NEG_START = -1e37


def din_attention(nc, ids, mask, target, emb, w1a, b1a, w2a, b2a, w1p, b1p, w2p, b2p, out):
    B, T = ids.shape
    V, D = emb.shape
    H = w1a.shape[1]
    G = B // P
    N = -(-T // BLOCK)
    K = G * N
    assert B == G * P and 2 * D == P and H == P and T % 2 == 0 and RING % 2 == 0

    with ExitStack() as ctx:
        def sb(name, shape, dt=F32):
            return ctx.enter_context(nc.sbuf_tensor(name, shape, dt))

        def psum(name, shape):
            return ctx.enter_context(nc.psum_tensor(name, shape, F32))

        def sem(name):
            return ctx.enter_context(nc.semaphore(name))

        raw_ids = sb("raw_ids", [P, G, T], I32)
        keys = sb("keys", [P, G, T])
        raw_target = sb("raw_target", [P, G], I32)
        wrap_target = sb("wrap_target", [P, G])
        target_idx = sb("target_idx", [P, G], U32)
        mask_u8 = sb("mask_u8", [P, G, T], mybir.dt.uint8)
        left = sb("left", [P, 2, T])
        top = sb("top", [P, 2, CHUNK])
        half_less_last = sb("half_less_last", [P, 2])
        signs = sb("signs", [P, 2, T])
        table_size = sb("table_size", [P, CHUNK])
        list_key = sb("list_key", [P, K * BLOCK])
        sign_sum = sb("sign_sum", [P, K * RING])
        copies = sb("copies", [P, RING])
        multiplicity = sb("multiplicity", [P, K * BLOCK])
        neg_bias = sb("neg_bias", [P, K * BLOCK])
        sum_left = sb("sum_left", [P, 1])
        all_keys = sb("all_keys", [P, G, T])
        ones = sb("ones", [P, 1])
        one_half = sb("one_half", [P, 1])
        more_left = sb("more_left", [1, N + 1], I32)
        saved_sum = sb("saved_sum", [P, G, D])
        saved_count = sb("saved_count", [P, G])
        saved_neg_max = sb("saved_neg_max", [P, G])
        ident = sb("ident", [P, P])
        w_feat = sb("w_feat", [P, H])
        w_diff = sb("w_diff", [D, H])
        w_target = sb("w_target", [D, H])
        wp_feat = sb("wp_feat", [P, H])
        wp_diff = sb("wp_diff", [D, H])
        wp_target = sb("wp_target", [D, H])
        w2a_row = sb("w2a_row", [P, H])
        w2p_sb = sb("w2p_sb", [H, 1])
        b1a_row = sb("b1a_row", [P, H])
        b1p_sb = sb("b1p_sb", [H, 1])
        b2a_sb = sb("b2a_sb", [P, 1])
        b2p_sb = sb("b2p_sb", [1, 1])
        t_rows = sb("t_rows", [P, G, D])
        t_cols = sb("t_cols", [D, G, P])
        c_row = sb("c_row", [P, G, H])

        idx = sb("idx", [P, BLOCK], U32)
        hist = sb("hist", [P, RING, CHUNK + 1, 2, D])
        neg_score = sb("neg_score", [P, RING, CHUNK + 1])
        prob = sb("prob", [P, RING, CHUNK + 1])
        count = sb("count", [P, RING, CHUNK + 1])
        prob_sum = sb("prob_sum", [P, CHUNK + 1])
        weighted = sb("weighted", [P, CHUNK + 1, D])
        feat = sb("feat", [P, 2, HALF, P])
        hidden = sb("hidden", [P, 2, HALF, H])
        relu_w2 = sb("relu_w2", [P, CHUNK, H])
        neg_dot = sb("neg_dot", [P, RING, CHUNK])

        denom = sb("denom", [P, 1])
        inv = sb("inv", [P, 1])
        t_over_sum = sb("t_over_sum", [P, D])
        user = sb("user", [P, G, 2, D])
        user_feat = sb("user_feat", [P, G, P])
        user_relu = sb("user_relu", [H, G, P])
        logits = sb("logits", [1, B])

        ps_h = psum("ps_h", [P, 2, HALF, P])
        ps_hidden = psum("ps_hidden", [P, 2, HALF, H])
        ps_misc = psum("ps_misc", [P, 512])
        ps_pred = psum("ps_pred", [P, 512])

        keys_step, keys_copied = sem("keys_step"), sem("keys_copied")
        top_ready, last_ready, removed = sem("top_ready"), sem("last_ready"), sem("removed")
        counted, lists_step = sem("counted"), sem("lists_step")
        keys_summed, left_sum, more_left_ready = sem("keys_summed"), sem("left_sum"), sem("more_left_ready")
        prob_counted, state_saved = sem("prob_counted"), sem("state_saved")
        target_in = sem("target_in")
        ids_in, mask_in = [sem("ids_in0"), sem("ids_in1")], [sem("mask_in0"), sem("mask_in1")]
        weights_in, out_stored = sem("weights_in"), sem("out_stored")
        zeroed, ident_ready = sem("zeroed"), sem("ident_ready")
        target_clamp = sem("target_clamp")
        target_idx_ready, targets_gathered = sem("target_idx_ready"), sem("targets_gathered")
        weights_folded, targets_transposed = sem("weights_folded"), sem("targets_transposed")
        t_cols_ready, c_row_product, c_row_ready = sem("t_cols_ready"), sem("c_row_product"), sem("c_row_ready")
        constants_ready, state_loaded = sem("constants_ready"), sem("state_loaded")
        waited = sem("waited")
        idx_staged = sem("idx_staged")
        gathered = [sem(f"gathered{q}") for q in range(2 * RING)]
        product_ready = sem("product_ready")
        h_transposed, feat_ready, hidden_product = sem("h_transposed"), sem("feat_ready"), sem("hidden_product")
        hidden_ready, dots_ready, w2a_negated = sem("hidden_ready"), sem("dots_ready"), sem("w2a_negated")
        neg_score_ready, max_ready, probs_ready = sem("neg_score_ready"), sem("max_ready"), sem("probs_ready")
        weighted_ready, sums_ready, denom_ready = sem("weighted_ready"), sem("sums_ready"), sem("denom_ready")
        t_scaled = sem("t_scaled")
        user_ready, user_transposed, user_feat_ready = sem("user_ready"), sem("user_transposed"), sem("user_feat_ready")
        pred_product, pred_relu_ready, logit_product = sem("pred_product"), sem("pred_relu_ready"), sem("logit_product")
        logits_ready = sem("logits_ready")

        WEIGHT_LOADS = 14
        block = ctx.enter_context(nc.Block())

        def needed(engine, level):
            return engine.value_load(more_left[0:1, bass.ds(level, 1)], min_val=0, max_val=1) != 0

        def further_levels(engine, compute):
            engine.wait_ge(more_left_ready, 1)
            with engine.If(needed(engine, 1)):
                with engine.Fori(1, N) as i:
                    with engine.If(needed(engine, i)):
                        compute(i)
                        engine.wait_ge(more_left_ready, i + 1)
                        engine.sem_inc(waited)

        @block.sync
        def _(sp):
            sp.dma_start(raw_target[:, :], target).then_inc(target_in, 16)
            for n, (lo, hi) in enumerate(((0, 1), (1, G))):
                rows = slice(lo * P, hi * P)
                sp.dma_start(raw_ids[:, lo:hi, :], ids[rows, :].rearrange("(g p) t -> p g t", p=P)
                             ).then_inc(ids_in[n], 16)
                sp.dma_start(mask_u8[:, lo:hi, :], mask[rows, :].rearrange("(g p) t -> p g t", p=P)
                             ).then_inc(mask_in[n], 16)
            for w1, feat_w, diff_w, target_w in ((w1a, w_feat, w_diff, w_target),
                                                 (w1p, wp_feat, wp_diff, wp_target)):
                sp.dma_start(feat_w[0:D, :], w1[0:D, :]).then_inc(weights_in, 16)
                sp.dma_start(target_w[:, :], w1[D:2 * D, :]).then_inc(weights_in, 16)
                sp.dma_start(diff_w[:, :], w1[2 * D:3 * D, :]).then_inc(weights_in, 16)
                sp.dma_start(feat_w[D:2 * D, :], w1[3 * D:4 * D, :]).then_inc(weights_in, 16)
            sp.dma_start(w2a_row[:, :], w2a.rearrange("h a -> a h").broadcast_to([P, H])).then_inc(weights_in, 16)
            sp.dma_start(w2p_sb[:, :], w2p).then_inc(weights_in, 16)
            sp.dma_start(b1a_row[:, :], b1a.rearrange("(a h) -> a h", a=1).broadcast_to([P, H])
                         ).then_inc(weights_in, 16)
            sp.dma_start(b1p_sb[:, :], b1p.rearrange("(h a) -> h a", a=1)).then_inc(weights_in, 16)
            sp.dma_start(b2a_sb[:, :], b2a.rearrange("(h a) -> h a", a=1).broadcast_to([P, 1])).then_inc(weights_in, 16)
            sp.dma_start(b2p_sb[:, :], b2p.rearrange("(h a) -> h a", a=1)).then_inc(weights_in, 16)
            sp.wait_ge(logits_ready, 2)
            further_levels(sp, lambda i: sp.wait_ge(logits_ready, (i + 1) * 2))
            sp.dma_start(out.rearrange("(a b) -> a b", a=1), logits[:, :]).then_inc(out_stored, 16)
            sp.wait_ge(out_stored, 16)

        @block.gpsimd
        def _(pool):
            nc.gpsimd.memset(ones[:, :], 1.0).then_inc(ident_ready, 1)
            nc.gpsimd.memset(one_half[:, :], 0.5).then_inc(ident_ready, 1)
            nc.gpsimd.memset(ident[:, :], 0.0).then_inc(zeroed, 1)
            pool.wait_ge(zeroed, 1)
            nc.gpsimd.affine_select(out=ident[:, :], in_=ident[:, :], compare_op=ALU.not_equal, fill=1.0,
                                    base=0, pattern=[[-1, P]], channel_multiplier=1).then_inc(ident_ready, 1)
            pool.wait_ge(target_idx_ready, 1)
            for g in range(G):
                pool.indirect_dma_start(t_rows[:, g, :], None, emb,
                                        bass.IndirectOffsetOnAxis(target_idx[:, g:g + 1], 0)
                                        ).then_inc(targets_gathered, 16)
            def gathers(k):
                for s in range(RING):
                    pool.wait_ge(idx_staged, k * RING + (s + 1))
                    pool.sem_inc(waited)
                    for j in range(CHUNK):
                        col = s * CHUNK + j
                        pool.indirect_dma_start(hist[:, s, j, 0, :], None, emb,
                                                bass.IndirectOffsetOnAxis(idx[:, col:col + 1], 0)
                                                ).then_inc(gathered[2 * s + j // HALF], 16)

            def level(i):
                with pool.Fori(0, G) as g:
                    gathers(i * G + g)

            level(0)
            further_levels(pool, level)

        @block.tensor
        def _(pe):
            pe.wait_ge(ident_ready, 3)
            pe.wait_ge(targets_gathered, 16 * G)
            for g in range(G):
                last = nc.tensor.transpose(ps_misc[0:D, g * P:(g + 1) * P], t_rows[:, g, :], ident[:, :])
            last.then_inc(targets_transposed, 1)
            def transposes(k, q):
                pe.wait_ge(product_ready, k * (2 * RING) + (q + 1))
                for j in range(HALF):
                    last = nc.tensor.transpose(
                        ps_h[:, q % 2, j, :],
                        hist[:, q // 2, q % 2 * HALF + j, :, :].rearrange("p a d -> p (a d)"), ident[:, :])
                last.then_inc(h_transposed, 1)

            transposes(0, 0)
            pe.wait_ge(weights_folded, 2)
            pe.wait_ge(t_cols_ready, 1)
            for g in range(G):
                last = nc.tensor.matmul(ps_pred[:, g * H:(g + 1) * H], t_cols[:, g, :], w_target[:, :],
                                        start=True, stop=True)
            last.then_inc(c_row_product, 1)

            def half_product(k, q, more):
                pe.wait_ge(feat_ready, k * (2 * RING) + (q + 1))
                for j in range(HALF):
                    last = nc.tensor.matmul(ps_hidden[:, q % 2, j, :], feat[:, q % 2, j, :], w_feat[:, :],
                                            start=True, stop=True)
                last.then_inc(hidden_product, 1)
                if q + 1 < 2 * RING:
                    transposes(k, q + 1)
                elif more:
                    transposes(k + 1, 0)

            def predict_users(i, lo, hi):
                pe.wait_ge(weights_folded, 4)
                pe.wait_ge(c_row_ready, 1)
                pe.wait_ge(user_ready, i * (2 * G) + 2 * hi)
                for g in range(lo, hi):
                    last = nc.tensor.transpose(ps_misc[:, g * P:(g + 1) * P],
                                               user[:, g, :, :].rearrange("p a d -> p (a d)"), ident[:, :])
                last.then_inc(user_transposed, 1)
                nc.tensor.matmul(ps_pred[:, lo * P:hi * P], wp_target[:, :],
                                 t_cols[:, lo:hi, :].rearrange("d g p -> d (g p)"), start=True, stop=False)

            def predict_hidden(lo, hi, n):
                pe.wait_ge(user_feat_ready, n + 1)
                nc.tensor.matmul(ps_pred[:, lo * P:hi * P], wp_feat[:, :],
                                 user_feat[:, lo:hi, :].rearrange("f g p -> f (g p)"),
                                 start=False, stop=True).then_inc(pred_product, 1)

            def predict_logits(lo, hi, n):
                pe.wait_ge(pred_relu_ready, n + 1)
                nc.tensor.matmul(ps_misc[0:1, lo * P:hi * P], w2p_sb[:, :],
                                 user_relu[:, lo:hi, :].rearrange("h g p -> h (g p)"),
                                 start=True, stop=True).then_inc(logit_product, 1)

            def level(i):
                with pe.Fori(0, G - 1) as g:
                    for q in range(2 * RING):
                        half_product(i * G + g, q, True)
                for q in range(2 * RING):
                    half_product(i * G + (G - 1), q, False)
                    if q == 0:
                        predict_users(i, 0, G - 1)
                    elif q == 1:
                        predict_hidden(0, G - 1, i * 2)
                    elif q == 3:
                        predict_logits(0, G - 1, i * 2)
                    elif q == 5:
                        pe.wait_ge(keys_summed, i + 1)
                        pe.wait_ge(logits_ready, i * 2 + 1)
                        nc.tensor.matmul(ps_misc[0:1, 0:1], sum_left[:, :], ones[:, :], start=True, stop=True
                                         ).then_inc(left_sum, 1)
                pe.wait_ge(more_left_ready, i + 1)
                predict_users(i, G - 1, G)
                predict_hidden(G - 1, G, i * 2 + 1)
                predict_logits(G - 1, G, i * 2 + 1)

            def further_level(i):
                transposes(i * G, 0)
                level(i)

            level(0)
            further_levels(pe, further_level)

        @block.scalar
        def _(act):
            act.wait_ge(ident_ready, 3)

            def scale_target(k, g):
                act.wait_ge(denom_ready, k * 2 + 2)
                nc.scalar.activation(t_over_sum[:, :], t_rows[:, bass.ds(g, 1), :].rearrange("p a d -> p (a d)"),
                                     ACT.Copy, scale=inv[:, 0:1]).then_inc(t_scaled, 1)

            def copy_keys(k, g):
                act.wait_ge(removed, k * RING)
                nc.scalar.copy(left[:, 0, :], keys[:, bass.ds(g, 1), :].rearrange("p a t -> p (a t)")
                               ).then_inc(keys_copied, 1)

            def list_entries(k, s):
                r, half = k * RING + s, s % 2
                act.wait_ge(top_ready, r + 1)
                nc.scalar.copy(list_key[:, bass.ds(k * BLOCK + s * CHUNK, CHUNK)], top[:, half, :]
                               ).then_inc(counted, 1)
                nc.scalar.activation(half_less_last[:, half:half + 1], top[:, half, CHUNK - 1:CHUNK], ACT.Identity,
                                     scale=-1.0, bias=one_half[:, 0:1]).then_inc(last_ready, 1)
                act.wait_ge(last_ready, r + 1)
                nc.scalar.activation(signs[:, half, :], left[:, half, :], ACT.Sign, bias=half_less_last[:, half:half + 1],
                                     accum_out=sign_sum[:, bass.ds(k * RING + s, 1)]).then_inc(counted, 1)

            def features(k, q):
                act.wait_ge(h_transposed, k * (2 * RING) + (q + 1))
                nc.scalar.copy(feat[:, q % 2, :, :], ps_h[:, q % 2, :, :]).then_inc(feat_ready, 1)

            def chunk(k, s, next_group, after_first=None, after_second=None):
                if s == 0 and next_group is not None:
                    copy_keys(k + 1, next_group)
                features(k, 2 * s + 1)
                if after_first is not None:
                    after_first()
                if s + 1 < RING:
                    features(k, 2 * s + 2)
                elif next_group is not None:
                    features(k + 1, 0)
                if after_second is not None:
                    after_second()
                act.wait_ge(max_ready, k * RING + (s + 1))
                nc.scalar.activation(prob[:, s, :], neg_score[:, s, :], ACT.Exp, scale=-1.0,
                                     bias=neg_score[:, (s + 1) % RING, CHUNK:CHUNK + 1]
                                     ).then_inc(probs_ready, 1)
                if next_group is not None:
                    list_entries(k + 1, s)

            def predict_users(lo, hi, n):
                act.wait_ge(user_transposed, n + 1)
                nc.scalar.copy(user_feat[:, lo:hi, :].rearrange("f g p -> f (g p)"), ps_misc[:, lo * P:hi * P]
                               ).then_inc(user_feat_ready, 1)

            def predict_hidden(lo, hi, n):
                act.wait_ge(pred_product, n + 1)
                nc.scalar.activation(user_relu[:, lo:hi, :].rearrange("h g p -> h (g p)"), ps_pred[:, lo * P:hi * P],
                                     ACT.Relu, bias=b1p_sb[:, 0:1]).then_inc(pred_relu_ready, 1)

            def predict_logits(lo, hi, n):
                act.wait_ge(logit_product, n + 1)
                nc.scalar.activation(logits[0:1, lo * P:hi * P], ps_misc[0:1, lo * P:hi * P], ACT.Identity,
                                     bias=b2p_sb[0:1, 0:1]).then_inc(logits_ready, 1)

            def level(i):
                for s in range(RING):
                    list_entries(i * G, s)
                features(i * G, 0)
                with act.Fori(0, G - 1) as g:
                    for s in range(RING):
                        chunk(i * G + g, s, g + 1)
                    scale_target(i * G + g, g)

                def sum_keys():
                    act.wait_ge(removed, (i * G + G) * RING)
                    nc.scalar.activation(all_keys[:, :, :].rearrange("p g t -> p (g t)"),
                                         keys[:, :, :].rearrange("p g t -> p (g t)"), ACT.Copy,
                                         accum_out=sum_left[:, :]).then_inc(keys_summed, 1)

                k = i * G + (G - 1)
                chunk(k, 0, None, lambda: predict_users(0, G - 1, i * 2), lambda: predict_hidden(0, G - 1, i * 2))
                chunk(k, 1, None, sum_keys, lambda: predict_logits(0, G - 1, i * 2))
                chunk(k, 2, None)
                chunk(k, 3, None)
                scale_target(k, G - 1)
                predict_users(G - 1, G, i * 2 + 1)
                predict_hidden(G - 1, G, i * 2 + 1)
                predict_logits(G - 1, G, i * 2 + 1)

            def further_level(i):
                copy_keys(i * G, 0)
                level(i)

            level(0)
            further_levels(act, further_level)

        @block.vector
        def _(dve):
            dve.wait_ge(target_in, 16)
            nc.vector.tensor_scalar(wrap_target[:, :], raw_target[:, :], 0, V, ALU.is_lt, ALU.mult
                                    ).then_inc(target_clamp, 1)
            dve.wait_ge(target_clamp, 1)
            nc.vector.tensor_tensor(wrap_target[:, :], wrap_target[:, :], raw_target[:, :], ALU.add
                                    ).then_inc(target_clamp, 1)
            dve.wait_ge(target_clamp, 2)
            nc.vector.tensor_scalar(target_idx[:, :], wrap_target[:, :], 0, V - 1, ALU.max, ALU.min
                                    ).then_inc(target_idx_ready, 1)

            flat_keys = keys[:, :, :].rearrange("p g t -> p (g t)")
            flat_ids = raw_ids[:, :, :].rearrange("p g t -> p (g t)")
            flat_mask = mask_u8[:, :, :].rearrange("p g t -> p (g t)")

            def make_keys(lo, hi, before):
                part = slice(lo * T, hi * T)
                nc.vector.tensor_scalar(flat_keys[:, part], flat_ids[:, part], 0, -V, ALU.is_lt, ALU.mult
                                        ).then_inc(keys_step, 1)
                dve.wait_ge(keys_step, before + 1)
                nc.vector.scalar_tensor_tensor(out=flat_keys[:, part], in0=flat_ids[:, part], scalar=-1.0,
                                               in1=flat_keys[:, part], op0=ALU.mult, op1=ALU.add
                                               ).then_inc(keys_step, 1)
                dve.wait_ge(keys_step, before + 2)
                nc.vector.tensor_scalar(flat_keys[:, part], flat_keys[:, part], 0, -(V - 1), ALU.min, ALU.max
                                        ).then_inc(keys_step, 1)
                dve.wait_ge(keys_step, before + 3)
                nc.vector.scalar_tensor_tensor(out=flat_keys[:, part], in0=flat_keys[:, part], scalar=float(V),
                                               in1=flat_mask[:, part], op0=ALU.add, op1=ALU.mult
                                               ).then_inc(keys_step, 1)
                dve.wait_ge(keys_step, before + 4)

            def list_round(k, s, g):
                r, half = k * RING + s, s % 2
                if s == 0:
                    dve.wait_ge(keys_copied, k + 1)
                    dve.sem_inc(waited)
                before = left[:, half, :]
                after = (left[:, (s + 1) % 2, :] if s + 1 < RING else
                         keys[:, bass.ds(g, 1), :].rearrange("p a t -> p (a t)"))
                nc.vector.max(top[:, half, :], before).then_inc(top_ready, 1)
                if not (isinstance(k, int) and r == 0):
                    dve.wait_ge(counted, r * 2)
                    dve.sem_inc(waited)
                dve.wait_ge(top_ready, r + 1)
                nc.vector.scalar_tensor_tensor(out=after, in0=before, scalar=top[:, half, CHUNK - 1:CHUNK],
                                               in1=before, op0=ALU.is_lt, op1=ALU.mult).then_inc(removed, 1)

            def stage(k, s):
                dve.wait_ge(removed, k * RING + (s + 1))
                nc.vector.scalar_tensor_tensor(out=idx[:, s * CHUNK:(s + 1) * CHUNK], in0=top[:, s % 2, :],
                                               scalar=1.0, in1=table_size[:, :], op0=ALU.max, op1=ALU.subtract,
                                               reverse1=True).then_inc(idx_staged, 1)

            def finish_lists(k):
                dve.wait_ge(counted, (k + 1) * (2 * RING))
                keys_of = list_key[:, bass.ds(k * BLOCK, BLOCK)]
                nc.vector.tensor_scalar(multiplicity[:, bass.ds(k * BLOCK, BLOCK)], keys_of, 0.0, None, ALU.is_gt
                                        ).then_inc(lists_step, 1)
                nc.vector.tensor_scalar(neg_bias[:, bass.ds(k * BLOCK, BLOCK)], keys_of, 0.0, -NEG_MASK,
                                        ALU.is_equal, ALU.mult).then_inc(lists_step, 1)
                nc.vector.tensor_scalar(copies[:, :], sign_sum[:, bass.ds(k * RING, RING)], 0.5,
                                        T / 2 - (CHUNK - 1), ALU.mult, ALU.add).then_inc(lists_step, 1)
                dve.wait_ge(lists_step, k * 4 + 3)
                lasts = multiplicity[:, bass.ds(k * BLOCK, BLOCK)].rearrange(
                    "p (c j) -> p c j", j=CHUNK)[:, :, CHUNK - 1]
                nc.vector.tensor_tensor(lasts, lasts, copies[:, :], ALU.mult).then_inc(lists_step, 1)
                dve.wait_ge(lists_step, (k + 1) * 4)
                dve.sem_inc(waited)

            def list_first_group(k):
                for s in range(RING):
                    list_round(k, s, 0)
                    stage(k, s)

            nc.vector.memset(table_size[:, :], float(V)).then_inc(constants_ready, 1)
            dve.wait_ge(constants_ready, 1)
            dve.wait_ge(ids_in[0], 16)
            dve.wait_ge(mask_in[0], 16)
            make_keys(0, 1, 0)
            nc.vector.tensor_copy(left[:, 0, :], keys[:, 0, :]).then_inc(keys_copied, 1)
            list_first_group(0)
            dve.wait_ge(ids_in[1], 16)
            dve.wait_ge(mask_in[1], 16)
            make_keys(1, G, 4)
            dve.wait_ge(targets_transposed, 1)
            nc.vector.tensor_copy(t_cols[:, :, :].rearrange("d g p -> d (g p)"), ps_misc[0:D, :]
                                  ).then_inc(t_cols_ready, 1)
            nc.vector.memset(count[:, :, :], 1.0).then_inc(constants_ready, 1)
            nc.vector.memset(saved_sum[:, :, :], 0.0).then_inc(constants_ready, 1)
            nc.vector.memset(saved_count[:, :], 0.0).then_inc(constants_ready, 1)
            nc.vector.memset(saved_neg_max[:, :], -NEG_START).then_inc(constants_ready, 1)
            nc.vector.memset(more_left[:, :], 0).then_inc(constants_ready, 1)
            dve.wait_ge(constants_ready, 6)

            def products(k, g, q):
                s, slots = q // 2, slice(q % 2 * HALF, (q % 2 + 1) * HALF)
                dve.wait_ge(gathered[q], (k + 1) * (16 * HALF))
                nc.vector.tensor_tensor(hist[:, s, slots, 1, :], hist[:, s, slots, 0, :],
                                        t_rows[:, bass.ds(g, 1), :].broadcast_to([P, HALF, D]),
                                        ALU.mult).then_inc(product_ready, 1)

            products(0, 0, 0)
            dve.wait_ge(weights_in, 16 * WEIGHT_LOADS)
            for feat_w, diff_w, target_w in ((w_feat, w_diff, w_target), (wp_feat, wp_diff, wp_target)):
                nc.vector.tensor_tensor(feat_w[0:D, :], feat_w[0:D, :], diff_w[:, :], ALU.add
                                        ).then_inc(weights_folded, 1)
                nc.vector.tensor_tensor(target_w[:, :], target_w[:, :], diff_w[:, :], ALU.subtract
                                        ).then_inc(weights_folded, 1)
            nc.vector.tensor_scalar(w2a_row[:, :], w2a_row[:, :], -1.0, None, ALU.mult).then_inc(w2a_negated, 1)
            dve.wait_ge(c_row_product, 1)
            nc.vector.tensor_tensor(c_row[:, :, :], ps_pred[:, :].rearrange("p (g h) -> p g h", g=G),
                                    b1a_row[:, :].unsqueeze(1).broadcast_to([P, G, H]), ALU.add
                                    ).then_inc(c_row_ready, 1)
            dve.wait_ge(c_row_ready, 1)
            dve.wait_ge(w2a_negated, 1)

            def half_scores(k, g, q):
                half, slot, done = q % 2, q % 2 * HALF, k * (2 * RING) + (q + 1)
                dve.wait_ge(hidden_product, done)
                nc.vector.tensor_tensor(hidden[:, half, :, :], ps_hidden[:, half, :, :],
                                        c_row[:, bass.ds(g, 1), :].broadcast_to([P, HALF, H]), ALU.add
                                        ).then_inc(hidden_ready, 1)
                dve.wait_ge(hidden_ready, done)
                for j in range(HALF):
                    last = nc.vector.scalar_tensor_tensor(
                        out=relu_w2[:, slot + j, :], in0=hidden[:, half, j, :], scalar=0.0,
                        in1=w2a_row[:, :], op0=ALU.max, op1=ALU.mult,
                        accum_out=neg_dot[:, q // 2, slot + j:slot + j + 1])
                last.then_inc(dots_ready, 1)

            def load_state(k, g):
                nc.vector.tensor_copy(hist[:, 0, CHUNK, 0, :], saved_sum[:, bass.ds(g, 1), :].rearrange(
                    "p a d -> p (a d)")).then_inc(state_loaded, 1)
                nc.vector.tensor_copy(count[:, 0, CHUNK:CHUNK + 1], saved_count[:, bass.ds(g, 1)]
                                      ).then_inc(state_loaded, 1)
                nc.vector.tensor_copy(neg_score[:, 0, CHUNK:CHUNK + 1], saved_neg_max[:, bass.ds(g, 1)]
                                      ).then_inc(state_loaded, 1)

            def softmax(k, g, s, next_group, between):
                done = k * RING + (s + 1)
                if s == 0:
                    dve.wait_ge(state_loaded, (k + 1) * 3)
                    dve.sem_inc(waited)
                dve.wait_ge(dots_ready, k * (2 * RING) + (2 * s + 2))
                nc.vector.scalar_tensor_tensor(
                    out=neg_score[:, s, 0:CHUNK], in0=neg_dot[:, s, :], scalar=b2a_sb[:, 0:1],
                    in1=neg_bias[:, bass.ds(k * BLOCK + s * CHUNK, CHUNK)], op0=ALU.subtract, op1=ALU.add
                    ).then_inc(neg_score_ready, 1)
                dve.wait_ge(neg_score_ready, done)
                nc.vector.tensor_reduce(neg_score[:, (s + 1) % RING, CHUNK:CHUNK + 1], neg_score[:, s, :],
                                        AX.X, ALU.min).then_inc(max_ready, 1)
                between()
                if next_group is not None:
                    list_round(k + 1, s, next_group)
                dve.wait_ge(probs_ready, done)
                nc.vector.tensor_tensor(prob[:, s, 0:CHUNK], prob[:, s, 0:CHUNK],
                                        multiplicity[:, bass.ds(k * BLOCK + s * CHUNK, CHUNK)], ALU.mult
                                        ).then_inc(prob_counted, 1)
                dve.wait_ge(prob_counted, done)
                nc.vector.tensor_tensor_reduce(
                    out=prob_sum[:, :], in0=prob[:, s, :], in1=count[:, s, :], scale=1.0, scalar=0.0,
                    op0=ALU.mult, op1=ALU.add,
                    accum_out=count[:, (s + 1) % RING, CHUNK:CHUNK + 1]).then_inc(sums_ready, 1)
                if s == RING - 1:
                    dve.wait_ge(sums_ready, done * 2 - 1)
                    nc.vector.tensor_scalar(denom[:, :], count[:, 0, CHUNK:CHUNK + 1], 1e-8, None, ALU.max
                                            ).then_inc(denom_ready, 1)
                nc.vector.tensor_tensor(weighted[:, :, :], hist[:, s, :, 0, :],
                                        prob[:, s, :].unsqueeze(2).broadcast_to([P, CHUNK + 1, D]), ALU.mult
                                        ).then_inc(weighted_ready, 1)
                if s == RING - 1:
                    dve.wait_ge(denom_ready, k * 2 + 1)
                    nc.vector.reciprocal(inv[:, :], denom[:, :]).then_inc(denom_ready, 1)
                dve.wait_ge(weighted_ready, done)
                nc.vector.tensor_reduce(hist[:, (s + 1) % RING, CHUNK, 0, :],
                                        weighted[:, :, :].rearrange("p j d -> p d j"),
                                        AX.X, ALU.add).then_inc(sums_ready, 1)
                dve.wait_ge(sums_ready, done * 2)

            def chunk(k, g, s, next_group):
                def next_products(q):
                    if q < 2 * RING:
                        products(k, g, q)
                    elif next_group is not None:
                        products(k + 1, next_group, q - 2 * RING)

                half_scores(k, g, 2 * s)
                next_products(2 * s + 2)
                if s == 0:
                    finish_lists(k)
                half_scores(k, g, 2 * s + 1)
                softmax(k, g, s, next_group, lambda: next_products(2 * s + 3))
                if next_group is not None:
                    stage(k + 1, s)

            def finish_block(k, g):
                dve.wait_ge(denom_ready, k * 2 + 2)
                nc.vector.tensor_scalar(user[:, bass.ds(g, 1), 0, :].rearrange("p a d -> p (a d)"),
                                        hist[:, 0, CHUNK, 0, :], inv[:, 0:1], None, ALU.mult
                                        ).then_inc(user_ready, 1)
                dve.wait_ge(t_scaled, k + 1)
                dve.sem_inc(waited)
                nc.vector.tensor_tensor(user[:, bass.ds(g, 1), 1, :].rearrange("p a d -> p (a d)"),
                                        hist[:, 0, CHUNK, 0, :], t_over_sum[:, :], ALU.mult
                                        ).then_inc(user_ready, 1)
                nc.vector.tensor_copy(saved_sum[:, bass.ds(g, 1), :].rearrange("p a d -> p (a d)"),
                                      hist[:, 0, CHUNK, 0, :]).then_inc(state_saved, 1)
                nc.vector.tensor_copy(saved_count[:, bass.ds(g, 1)], count[:, 0, CHUNK:CHUNK + 1]
                                      ).then_inc(state_saved, 1)
                nc.vector.tensor_copy(saved_neg_max[:, bass.ds(g, 1)], neg_score[:, 0, CHUNK:CHUNK + 1]
                                      ).then_inc(state_saved, 1)
                dve.wait_ge(state_saved, (k + 1) * 3)
                dve.sem_inc(waited)

            def level(i):
                products(i * G, 0, 1)
                with dve.Fori(0, G - 1) as g:
                    load_state(i * G + g, g)
                    for s in range(RING):
                        chunk(i * G + g, g, s, g + 1)
                    finish_block(i * G + g, g)
                k = i * G + (G - 1)
                load_state(k, G - 1)
                chunk(k, G - 1, 0, None)
                chunk(k, G - 1, 1, None)
                chunk(k, G - 1, 2, None)
                dve.wait_ge(left_sum, i + 1)
                nc.vector.tensor_scalar(more_left[0:1, bass.ds(i + 1, 1)], ps_misc[0:1, 0:1], 0.0, None, ALU.is_gt
                                        ).then_inc(more_left_ready, 1)
                chunk(k, G - 1, 3, None)
                finish_block(k, G - 1)

            def further_level(i):
                list_first_group(i * G)
                products(i * G, 0, 0)
                level(i)

            level(0)
            further_levels(dve, further_level)


def kernel(**inputs):
    import numpy as np
    import concourse.bacc as bacc
    from concourse import mybir as mb
    from concourse.bass_utils import run_bass_kernel_spmd

    nc = bacc.Bacc("TRN2", target_bir_lowering=False, num_devices=1)
    order = ["r_history_ids", "r_history_mask", "r_target_ids", "L0_rec_emb", "L0_rec_W1a", "L0_rec_b1a",
             "L0_rec_W2a", "L0_rec_b2a", "L0_rec_W1p", "L0_rec_b1p", "L0_rec_W2p", "L0_rec_b2p"]
    arrays, args = {}, []
    for name in order:
        a = np.ascontiguousarray(inputs[name])
        if name == "r_target_ids":
            a = np.ascontiguousarray(a.reshape(-1, P).T)
        arrays[name] = a
        args.append(nc.dram_tensor(name, a.shape, mb.dt.from_np(a.dtype), kind="ExternalInput").ap())
    out = nc.dram_tensor("logits_out", (inputs["r_target_ids"].shape[0],), mb.dt.float32,
                         kind="ExternalOutput").ap()
    din_attention(nc, *args, out)
    r = run_bass_kernel_spmd(nc, [arrays], core_ids=[0])
    return r.results[0]["logits_out"]
```
